# Optimizing a Trainium2 kernel written in Bass

```python
import numpy as np
import jax
import jax.numpy as jnp

def _softmax(x, axis=-1):
    return jax.nn.softmax(x, axis=axis)

def _gelu(x):
    return jax.nn.gelu(x, approximate=True)

def _silu(x):
    return jax.nn.silu(x)

def _sigmoid(x):
    return jax.nn.sigmoid(x)

def _layernorm(x, axis=-1, eps=1e-05):
    m = jnp.mean(x, axis=axis, keepdims=True)
    v = jnp.var(x, axis=axis, keepdims=True)
    return (x - m) / jnp.sqrt(v + eps)

def _scatter_add(tgt, idx, src, axis=0):
    return tgt.at[idx].add(src)

def _segment_sum(src, seg, n):
    return jax.ops.segment_sum(src, seg, n)
kernel_name = 'mk_adaln_d1_jaxref_r8_b1b5b4'

def setup_inputs(seed: int=0):
    np.random.seed(seed)
    _w = jnp.asarray

    def _L0_attn_setup():
        import jax, jax.numpy as jnp
        import numpy as np
        D_MODEL, D_STATE, D_CONV, EXPAND = (128, 16, 4, 2)
        D_INNER = EXPAND * D_MODEL
        B, L = (2, 512)
        LN_EPS = 1e-05

        def _layernorm(x, gamma, beta):
            mu = jnp.mean(x, axis=-1, keepdims=True)
            var = jnp.mean(jnp.square(x - mu), axis=-1, keepdims=True)
            return (x - mu) * jax.lax.rsqrt(var + LN_EPS) * gamma + beta

        def _causal_depthwise_conv(xp, conv_w, conv_b):
            lhs = jnp.pad(xp.transpose(0, 2, 1), ((0, 0), (0, 0), (D_CONV - 1, 0)))
            out = jax.lax.conv_general_dilated(lhs, conv_w, window_strides=(1,), padding='VALID', dimension_numbers=('NCH', 'OIH', 'NCH'), feature_group_count=D_INNER)
            return out.transpose(0, 2, 1) + conv_b
        key = jax.random.key(seed)
        ks = jax.random.split(key, 6)
        x = jax.random.normal(ks[0], (B, L, D_MODEL), dtype=jnp.float32)
        ln_gamma = jnp.ones((D_MODEL,), jnp.float32)
        ln_beta = jnp.zeros((D_MODEL,), jnp.float32)
        W_in = jax.random.normal(ks[1], (2 * D_INNER, D_MODEL), jnp.float32) / np.sqrt(D_MODEL).astype(np.float32)
        conv_w = jax.random.normal(ks[2], (D_INNER, 1, D_CONV), jnp.float32) * 0.1
        conv_b = jnp.zeros((D_INNER,), jnp.float32)
        W_out = jax.random.normal(ks[3], (D_MODEL, D_INNER), jnp.float32) / np.sqrt(D_INNER).astype(np.float32)
        A = jnp.eye(D_STATE, dtype=jnp.float32)
        Bm = jax.random.normal(ks[4], (D_STATE, D_INNER), jnp.float32) * 0.01
        Cm = jax.random.normal(ks[5], (D_STATE, D_INNER), jnp.float32) * 0.01
        return dict(x=x, ln_gamma=ln_gamma, ln_beta=ln_beta, W_in=W_in, conv_w=conv_w, conv_b=conv_b, W_out=W_out, A=A, Bm=Bm, Cm=Cm)
    _L0_attn_in = _L0_attn_setup()

    def _L0_ffn_setup():
        import jax, jax.numpy as jnp
        import numpy as np
        import math
        B, S, D = (4, 256, 128)
        E, DFF = (16, 256)
        CAP_FACTOR = 2.0
        ROUTER_HIDDEN = 128
        CAPACITY = int(math.ceil(S * CAP_FACTOR / E))
        key = jax.random.key(seed)
        ks = jax.random.split(key, 6)

        def uinit(k, shape, fan_in):
            bound = math.sqrt(3.0) * math.sqrt(1.0 / 3.0) / math.sqrt(fan_in)
            return jax.random.uniform(k, shape, jnp.float32, -bound, bound)
        return {'hidden_states': jax.random.normal(ks[0], (B, S, D), jnp.float32), 'router_w1': jax.random.normal(ks[1], (D, ROUTER_HIDDEN), jnp.float32) / math.sqrt(D), 'router_w2': jax.random.normal(ks[2], (ROUTER_HIDDEN, E), jnp.float32) / math.sqrt(ROUTER_HIDDEN), 'w1': uinit(ks[3], (E, D, DFF), D), 'w2': uinit(ks[4], (E, D, DFF), D), 'w3': uinit(ks[5], (E, DFF, D), DFF)}
    _L0_ffn_in = _L0_ffn_setup()
    _L0_c = _w((lambda *s: np.random.randn(*s).astype(np.float32) * 0.05)(4, 128))
    _L0_wmod = _w((lambda *s: np.random.randn(*s).astype(np.float32) * 0.05)(128, 6 * 128) * 128 ** (-0.5))
    _d = {'L0_attn_x': _L0_attn_in['x'], 'L0_attn_ln_gamma': _L0_attn_in['ln_gamma'], 'L0_attn_ln_beta': _L0_attn_in['ln_beta'], 'L0_attn_W_in': _L0_attn_in['W_in'], 'L0_attn_conv_w': _L0_attn_in['conv_w'], 'L0_attn_conv_b': _L0_attn_in['conv_b'], 'L0_attn_W_out': _L0_attn_in['W_out'], 'L0_attn_A': _L0_attn_in['A'], 'L0_attn_Bm': _L0_attn_in['Bm'], 'L0_attn_Cm': _L0_attn_in['Cm'], 'L0_ffn_router_w1': _L0_ffn_in['router_w1'], 'L0_ffn_router_w2': _L0_ffn_in['router_w2'], 'L0_ffn_w1': _L0_ffn_in['w1'], 'L0_ffn_w2': _L0_ffn_in['w2'], 'L0_ffn_w3': _L0_ffn_in['w3'], 'L0_c': _L0_c, 'L0_wmod': _L0_wmod}
    _x0 = _d['L0_attn_x']
    _d['L0_attn_x'] = jax.random.normal(jax.random.fold_in(jax.random.key(seed), 1), (4, 1024, 128), dtype=_x0.dtype)
    del _x0
    return _d

def reference(L0_attn_x, L0_attn_ln_gamma, L0_attn_ln_beta, L0_attn_W_in, L0_attn_conv_w, L0_attn_conv_b, L0_attn_W_out, L0_attn_A, L0_attn_Bm, L0_attn_Cm, L0_ffn_router_w1, L0_ffn_router_w2, L0_ffn_w1, L0_ffn_w2, L0_ffn_w3, L0_c, L0_wmod):

    def _L0_attn_ref(x, ln_gamma, ln_beta, W_in, conv_w, conv_b, W_out, A, Bm, Cm):
        import jax, jax.numpy as jnp
        import numpy as np
        D_MODEL, D_STATE, D_CONV, EXPAND = (128, 16, 4, 2)
        D_INNER = EXPAND * D_MODEL
        B, L = (2, 512)
        LN_EPS = 1e-05

        def _layernorm(x, gamma, beta):
            mu = jnp.mean(x, axis=-1, keepdims=True)
            var = jnp.mean(jnp.square(x - mu), axis=-1, keepdims=True)
            return (x - mu) * jax.lax.rsqrt(var + LN_EPS) * gamma + beta

        def _causal_depthwise_conv(xp, conv_w, conv_b):
            lhs = jnp.pad(xp.transpose(0, 2, 1), ((0, 0), (0, 0), (D_CONV - 1, 0)))
            out = jax.lax.conv_general_dilated(lhs, conv_w, window_strides=(1,), padding='VALID', dimension_numbers=('NCH', 'OIH', 'NCH'), feature_group_count=D_INNER)
            return out.transpose(0, 2, 1) + conv_b
        xn = _layernorm(x, ln_gamma, ln_beta)
        xz = jnp.einsum('bld,ed->ble', xn, W_in)
        x_part, z = jnp.split(xz, 2, axis=-1)
        x_conv = jax.nn.silu(_causal_depthwise_conv(x_part, conv_w, conv_b))
        u_seq = x_part.transpose(1, 0, 2)
        xc_seq = x_conv.transpose(1, 0, 2)
        z_seq = z.transpose(1, 0, 2)

        def step(state, inp):
            u_t, xc_t, z_t = inp
            state = state @ A.T + u_t @ Bm.T
            out = (xc_t + state @ Cm) * jax.nn.sigmoid(z_t)
            return (state, out)
        state0 = jnp.zeros((x.shape[0], D_STATE), x.dtype)
        _, ys = jax.lax.scan(step, state0, (u_seq, xc_seq, z_seq))
        y = ys.transpose(1, 0, 2)
        residual = jnp.einsum('bli,di->bld', y, W_out)
        return x + residual

    def _L0_ffn_ref(hidden_states, router_w1, router_w2, w1, w2, w3):
        import jax, jax.numpy as jnp
        import numpy as np
        import math
        B, S, D = (4, 256, 128)
        E, DFF = (16, 256)
        CAP_FACTOR = 2.0
        ROUTER_HIDDEN = 128
        CAPACITY = int(math.ceil(S * CAP_FACTOR / E))
        b, s, d = hidden_states.shape
        e = w1.shape[0]
        cap = CAPACITY
        router_logits = jax.nn.silu(hidden_states @ router_w1) @ router_w2
        expert_probs = jax.nn.softmax(router_logits.transpose(0, 2, 1), axis=-1)
        expert_weights, token_indices = jax.lax.top_k(expert_probs, cap)
        expert_weights = expert_weights / (expert_weights.sum(-1, keepdims=True) + 1e-09)
        expert_inputs = jax.vmap(lambda h, i: h[i])(hidden_states, token_indices)
        gate = jax.nn.silu(jnp.einsum('becd,edf->becf', expert_inputs, w1))
        value = jnp.einsum('becd,edf->becf', expert_inputs, w2)
        expert_out = jnp.einsum('becf,efd->becd', gate * value, w3)
        weighted = expert_out * expert_weights[..., None]

        def combine(idx, vals):
            return jnp.zeros((s, d), vals.dtype).at[idx.reshape(-1)].add(vals.reshape(-1, d))
        output = jax.vmap(combine)(token_indices, weighted)
        return output
    x = L0_attn_x
    mod = (_silu(L0_c) @ L0_wmod).reshape(L0_c.shape[0], 6, 1, -1)
    sa, ca, ga, sb, cb, gb = (mod[:, 0], mod[:, 1], mod[:, 2], mod[:, 3], mod[:, 4], mod[:, 5])
    ga = (2 * (ga >= 0) - 1) * jnp.maximum(jnp.abs(ga), 0.25)
    gb = (2 * (gb >= 0) - 1) * jnp.maximum(jnp.abs(gb), 0.25)
    h = _layernorm(x, axis=-1) * (1 + ca) + sa
    x = x + ga * _L0_attn_ref(h, L0_attn_ln_gamma, L0_attn_ln_beta, L0_attn_W_in, L0_attn_conv_w, L0_attn_conv_b, L0_attn_W_out, L0_attn_A, L0_attn_Bm, L0_attn_Cm)
    h = _layernorm(x, axis=-1) * (1 + cb) + sb
    x = x + gb * _L0_ffn_ref(h, L0_ffn_router_w1, L0_ffn_router_w2, L0_ffn_w1, L0_ffn_w2, L0_ffn_w3)
    return x

_drawn_inputs = setup_inputs


def setup_inputs(seed=0):
    import zlib

    import numpy as np

    out = dict(_drawn_inputs(seed))
    spreads = {'L0_attn_ln_gamma': (1.0, 0.6),
     'L0_attn_ln_beta': (0.0, 0.1),
     'L0_attn_conv_b': (0.0, 0.8)}
    factors = {'L0_attn_conv_w': 3.843,
     'L0_ffn_router_w1': 8.0,
     'L0_ffn_router_w2': 8.0,
     'L0_ffn_w1': 8.0,
     'L0_ffn_w2': 8.0,
     'L0_ffn_w3': 8.0}
    for name, (base, spread) in spreads.items():
        noise = np.random.default_rng([zlib.crc32(name.encode()), seed]).standard_normal(out[name].shape)
        drawn = base * np.exp(spread * noise) if base else spread * noise
        out[name] = jnp.asarray(drawn.astype(out[name].dtype))
    for name, factor in factors.items():
        out[name] = (out[name] * factor).astype(out[name].dtype)
    return out
```

```python
from contextlib import ExitStack

import concourse.bass as bass
from concourse import mybir

F32 = mybir.dt.float32
BF16 = mybir.dt.bfloat16
U32 = mybir.dt.uint32
ALU = mybir.AluOpType
ACT = mybir.ActivationFunctionType

P = 128
STEPS = 8
LN_EPS = 1e-5
CAPACITY = 32
CONV_TAPS = 4
LOWEST = -3.4028234e38


class Order:

    def __init__(self, eng, sem):
        self.eng, self.sem, self.at = eng, sem, 0

    def after(self, ins):
        self.at += 1
        ins.then_inc(self.sem, 1)
        self.eng.wait_ge(self.sem, self.at)


def adaln_block(nc, x, vectors, w_mod, w_in_t, w_in_x, w_out_t, a_pair, c_m, b_m_t, router_w1,
                router_w2, w1, w2, w3, out):
    B, L, D = x.shape
    CH = L // STEPS
    INNER = w_in_t.shape[1] // 2
    M = INNER // P
    S = a_pair.shape[0]
    E, _, DFF = w1.shape
    FH = DFF // P
    G = 4
    NG = E // G
    HALF = STEPS // 2
    W = HALF * CH
    UNITS = 2 * B
    SLOTS = 8
    PAD = (STEPS - 1) * S
    assert CH == P and D == P and M == 2 and STEPS * S == P and G * CAPACITY == P and W == 512
    assert B == 4 and CH == 2 * STEPS * STEPS and E <= 32

    x_rows = x.rearrange("b (c j) d -> b c (j d)", j=STEPS)
    out_rows = out.rearrange("b (c j) d -> b c (j d)", j=STEPS)
    norm_rows = nc.dram_tensor("norm_rows", [B * L, D], F32, kind="Internal").ap()
    norm_by_chunk = norm_rows.rearrange("(b c j) d -> b c (j d)", b=B, j=STEPS)

    with ExitStack() as ctx:
        def sb(name, shape, dt=F32):
            return ctx.enter_context(nc.sbuf_tensor(name, shape, dt))

        def sem(name):
            return ctx.enter_context(nc.semaphore(name))

        bank = [ctx.enter_context(nc.psum_tensor(f"bank{i}", [P, W], F32)) for i in range(8)]

        ident = sb("ident", [P, P])
        ones = sb("ones", [P, P])
        minus_half = sb("minus_half", [P, STEPS])
        batch_row = sb("batch_row", [P, NG, B])
        select_last = sb("select_last", [S, P])
        vec = sb("vec", [P, vectors.shape[1]])
        cond = vec[:, 0:4]
        gamma, beta = vec[:, 4:5], vec[:, 5:6]
        conv_b = vec[:, 6:8]
        conv_w = vec[:, 8:16]
        win_t = sb("win_t", [P, 2 * INNER])
        win_x = sb("win_x", [P, M, D])
        wout_t = sb("wout_t", [P, M, D])
        apair = sb("apair", [S, 2, S])
        bm_t = sb("bm_t", [P, M, S])
        c_block = sb("c_block", [P, STEPS, INNER])
        r1 = sb("r1", [P, P])
        r2 = sb("r2", [P, 32])
        experts = sb("experts", [P, SLOTS, 2 * DFF + FH * D])

        cond_s = sb("cond_s", [P, B])
        shift_a = sb("shift_a", [P, B, D])
        scale_a = sb("scale_a", [P, B, D])
        gates = sb("gates", [P, B, 2 * D])
        mod_b = sb("mod_b", [P, 2, B])
        wout_g = sb("wout_g", [P, B, M, D])

        powers = sb("powers", [S, 3, (STEPS + 1) * S])
        plain = sb("plain", [S, 3, 4, S])
        bin_w = sb("bin_w", [S, D])
        into_pad = sb("into_pad", [P, PAD + P])
        last_pad = sb("last_pad", [P, 2, PAD + P])
        y1 = sb("y1", [P, B, CH])
        y2 = sb("y2", [P, B, 16])
        y3 = sb("y3", [P, B, 2])
        carry3 = sb("carry3", [S, B])
        carry2 = sb("carry2", [S, B, 16])
        carry1 = sb("carry1", [S, B, CH])

        xs = sb("xs", [P, B, STEPS, D])
        hs = sb("hs", [P, B, STEPS, D])
        xhat = sb("xhat", [P, STEPS, D])
        xn = sb("xn", [P, STEPS, D])
        xn_t = sb("xn_t", [P, 2, STEPS, CH])
        u = sb("u", [P, M, STEPS, CH + 1])
        conv = sb("conv", [P, M, B, STEPS * CH])
        gate_z = sb("gate_z", [P, M, B, STEPS * CH])
        y = sb("y", [P, 2, M, W])
        early = y[:, :, :, :].rearrange("p a m t -> p (a m t)")
        wmod = early[:, 0:6 * D]
        cond_rows = early[:, 6 * D:(6 + B) * D].rearrange("p (b t) -> p b t", b=B)
        gate_sign = early[:, 10 * D:12 * D]
        gate_size = early[:, 12 * D:14 * D]
        token_of = xn_t[:, 0]
        xhat3 = sb("xhat3", [P, 2, HALF, D])
        h2_t = sb("h2_t", [P, 2, W])
        routed = xs
        st1 = sb("st1", [P, STEPS, 6])
        st2 = sb("st2", [P, STEPS, 6])
        tmp = sb("tmp", [P, 4, STEPS])
        mean = sb("mean", [P, 3, B, STEPS])
        var = sb("var", [P, 3, B, STEPS])
        rstd = sb("rstd", [P, 3, B, STEPS])

        logits = sb("logits", [P, CH, STEPS])
        left = xn[:, :, :].rearrange("p j d -> p (j d)")
        exps = xhat[:, :, :].rearrange("p j d -> p (j d)")
        top = sb("top", [P, CAPACITY])
        top_at = sb("top_at", [P, CAPACITY], U32)
        top_at_f = sb("top_at_f", [P, CAPACITY])
        neg_max = sb("neg_max", [P, 1])
        exp_all = sb("exp_all", [P, 1])
        exp_top = sb("exp_top", [P, 1])
        e_top = sb("e_top", [P, CAPACITY])
        rz = sb("rz", [P, 1])
        den = sb("den", [P, 1])
        rden = sb("rden", [P, 1])
        w_top = sb("w_top", [P, CAPACITY])
        slot_at = sb("slot_at", [P, 2, NG * B])
        slot_row = sb("slot_row", [P, NG * B], U32)

        def over(base, at, dt, *shape):
            n = 1
            for d in shape:
                n *= d
            flat = base[:, :, :, :].rearrange("p m b t -> p (m b t)")
            size = 2 if dt == BF16 else 4
            ap = flat[:, at // 4:(at + n * size) // 4]
            ap = ap if dt == F32 else ap.bitcast(dt)
            names = "abcdef"[:len(shape)]
            return ap.rearrange(f"p ({' '.join(names)}) -> p {' '.join(names)}",
                                **dict(zip(names[1:], shape[1:]))), at + n * size

        onehot, _ = over(conv, 0, BF16, NG, B, STEPS * CH)
        picked, at = over(gate_z, 0, F32, NG, B, D)
        picked_t, at = over(gate_z, at, F32, 2, G, B, CAPACITY)
        silu_g, at = over(gate_z, at, F32, 2, FH * P)
        hidden = xn_t[:, 1].rearrange("p (q f) t -> p q f t", q=G)
        value, at = over(gate_z, at, F32, B, D)
        rest, at = over(gate_z, at, F32, B, D)
        parts, at = over(gate_z, at, BF16, NG, 3, B, D)

        in_x = [sem(f"in_x{b}") for b in range(B)]
        in_vec, in_wmod, in_win, in_winx, in_wout, in_a, in_bm = (
            sem(n) for n in ("in_vec", "in_wmod", "in_win", "in_winx", "in_wout", "in_a", "in_bm"))
        in_c, in_r1, in_r2 = sem("in_c"), sem("in_r1"), sem("in_r2")
        in_expert = [sem(f"in_expert{i}") for i in range(SLOTS)]
        const_ready = sem("const_ready")
        pool_order, dve_order, act_order = sem("pool_order"), sem("dve_order"), sem("act_order")
        ones_ready = sem("ones_ready")
        cond_ready = sem("cond_ready")
        cond_rows_ready = sem("cond_rows_ready")
        mod_mm = sem("mod_mm")
        mod_ready = sem("mod_ready")
        gates_ready = sem("gates_ready")
        wout_ready = sem("wout_ready")
        pow_mm, pow_ready = sem("pow_mm"), sem("pow_ready")
        var_ready, rstd_ready = sem("var_ready"), sem("rstd_ready")
        xhat_ready, h_ready, xn_ready = sem("xhat_ready"), sem("h_ready"), sem("xn_ready")
        base_ready = sem("base_ready")
        tr_done, xnt_ready = sem("tr_done"), sem("xnt_ready")
        xz_mm, u_ready, xz_read = sem("xz_mm"), sem("u_ready"), sem("xz_read")
        scan_in = sem("scan_in")
        conv_done, silu_done = sem("conv_done"), sem("silu_done")
        scan_mm, scan_step = sem("scan_mm"), sem("scan_step")
        state_ready = sem("state_ready")
        sc_mm, sc_read, y_ready = sem("sc_mm"), sem("sc_read"), sem("y_ready")
        out_mm, x1_ready = sem("out_mm"), sem("x1_ready")
        xhat3_ready, stored = sem("xhat3_ready"), [sem("stored0"), sem("stored1")]
        tr3_done, h2_ready, router_mm, routed_ready = (
            sem("tr3_done"), sem("h2_ready"), sem("router_mm"), sem("routed_ready"))
        logits_mm, logits_ready = sem("logits_mm"), sem("logits_ready")
        max_ready, exp_ready, top_ready, weights_ready = (
            sem("max_ready"), sem("exp_ready"), sem("top_ready"), sem("weights_ready"))
        slots_mm, slots_ready = sem("slots_mm"), sem("slots_ready")
        picked_in = [sem(f"picked_in{g}") for g in range(NG)]
        ptr_done, pickt_ready = sem("ptr_done"), sem("pickt_ready")
        ffn_mm, silu_g_ready, hidden_ready = sem("ffn_mm"), sem("silu_g_ready"), sem("hidden_ready")
        eout_mm, value_ready = sem("eout_mm"), sem("value_ready")
        hi_ready, mid_ready, lo_ready, rest_ready = (
            sem("hi_ready"), sem("mid_ready"), sem("lo_ready"), sem("rest_ready"))
        onehot_ready = sem("onehot_ready")
        scatter_mm, final_ready = sem("scatter_mm"), sem("final_ready")
        out_stored = sem("out_stored")

        tr_bank = bank[0:2]
        xz_bank = bank[2:6]
        y_bank, small_bank = bank[6], bank[7]
        sc_bank, out_bank, tr3_bank, router_bank = bank[2:4], bank[4], bank[0], bank[1]
        logit_bank = bank[5:7]
        ptr_bank, slot_bank, ffn_bank, eout_bank = bank[0], (bank[1], bank[7]), bank[2:4], bank[4]
        scatter_bank = [bank[5], bank[6], bank[7]]

        block = ctx.enter_context(nc.Block())

        @block.sync
        def _(sp):
            sp.dma_start(vec[:, :], vectors).then_inc(in_vec, 16)
            sp.dma_start(xs[:, 0], x_rows[0]).then_inc(in_x[0], 16)
            sp.dma_start(wmod[:, :], w_mod).then_inc(in_wmod, 16)
            sp.dma_start(apair[:, :, :], a_pair).then_inc(in_a, 16)
            sp.dma_start(win_t[:, :], w_in_t).then_inc(in_win, 16)
            sp.dma_start(xs[:, 1], x_rows[1]).then_inc(in_x[1], 16)
            sp.dma_start(bm_t[:, :, :], b_m_t).then_inc(in_bm, 16)
            sp.dma_start(win_x[:, :, :], w_in_x).then_inc(in_winx, 16)
            for b in range(2, B):
                sp.dma_start(xs[:, b], x_rows[b]).then_inc(in_x[b], 16)
            sp.dma_start(wout_t[:, :, :], w_out_t).then_inc(in_wout, 16)
            sp.dma_start(r1[:, :], router_w1).then_inc(in_r1, 16)
            sp.wait_ge(const_ready, 4)
            for j in range(STEPS):
                sp.dma_start(c_block[S * j:S * (j + 1), j, :], c_m).then_inc(in_c, 16)
            sp.dma_start(r2[:, 0:E], router_w2).then_inc(in_r2, 16)

            def load_expert(e):
                s = e % SLOTS
                sp.dma_start(experts[:, s, 0:DFF], w1[e]).then_inc(in_expert[s], 16)
                sp.dma_start(experts[:, s, DFF:2 * DFF], w2[e]).then_inc(in_expert[s], 16)
                sp.dma_start(experts[:, s, 2 * DFF:].rearrange("p (f d) -> p f d", f=FH), w3[e]).then_inc(
                    in_expert[s], 16)

            for e in range(SLOTS):
                load_expert(e)
            for n in range(UNITS):
                b, hf = n // 2, n % 2
                sp.wait_ge(xhat3_ready, n + 1)
                sp.dma_start(norm_by_chunk[b][:, hf * W:(hf + 1) * W],
                             xhat3[:, hf].rearrange("p j d -> p (j d)")).then_inc(stored[hf], 16)
            for e in range(SLOTS, E):
                if e % G == 0:
                    sp.wait_ge(eout_mm, (e - SLOTS) // G + 1)
                load_expert(e)
            for n in range(UNITS):
                b, hf = n // 2, n % 2
                sp.wait_ge(final_ready, n + 1)
                sp.dma_start(out_rows[b][:, hf * W:(hf + 1) * W],
                             hs[:, b, hf * HALF:(hf + 1) * HALF, :].rearrange("p j d -> p (j d)")
                             ).then_inc(out_stored, 16)
            sp.wait_ge(out_stored, 16 * UNITS)

        @block.gpsimd
        def _(pool):
            order = Order(pool, pool_order)
            order.after(pool.memset(ident[:, :], 0.0))
            pool.affine_select(out=ident[:, :], in_=ident[:, :], compare_op=ALU.not_equal, fill=1.0, base=0,
                               pattern=[[-1, P]], channel_multiplier=1).then_inc(const_ready, 1)
            pool.memset(minus_half[:, :], -0.5).then_inc(const_ready, 1)

            def power(kind, b, j0, n, count):
                pool.wait_ge(var_ready, count)
                pool.tensor_tensor(rstd[:, kind, b, j0:j0 + n], var[:, kind, b, j0:j0 + n],
                                   minus_half[:, 0:n], ALU.pow).then_inc(rstd_ready, 1)

            pool.memset(r2[:, :], 0.0).then_inc(const_ready, 1)
            pool.memset(c_block[:, :, :], 0.0).then_inc(const_ready, 1)
            pool.memset(into_pad[:, 0:PAD], 0.0).then_inc(const_ready, 1)
            pool.memset(last_pad[:, :, 0:PAD], 0.0).then_inc(const_ready, 1)
            order.after(pool.memset(select_last[:, :], 0.0))
            pool.affine_select(out=select_last[:, :], in_=select_last[:, :], compare_op=ALU.not_equal,
                               fill=1.0, base=PAD, pattern=[[-1, P]], channel_multiplier=1
                               ).then_inc(const_ready, 1)
            power(0, 0, 0, STEPS, 1)
            pool.memset(u[:, :, :, 0:1], 0.0).then_inc(const_ready, 1)
            pool.memset(carry2[:, :, 0:1], 0.0).then_inc(const_ready, 1)
            pool.memset(carry1[:, :, 0:1], 0.0).then_inc(const_ready, 1)

            def per_row(table, b):
                return table[:, b, 0:D].unsqueeze(1).to_broadcast([P, STEPS, D])

            def base(b):
                pool.wait_ge(xn_ready, 2 * (b + 1))
                pool.wait_ge(gates_ready, B)
                order.after(pool.tensor_tensor(hs[:, b], hs[:, b], per_row(gates, b), ALU.mult))
                pool.tensor_tensor(hs[:, b], hs[:, b], xs[:, b], ALU.add).then_inc(base_ready, 1)

            for b in range(B):
                pool.wait_ge(xhat_ready, b + 1)
                pool.wait_ge(mod_ready, b + 1)
                order.after(pool.tensor_tensor(hs[:, b], xhat[:, :, :], per_row(scale_a, b), ALU.mult))
                pool.tensor_tensor(hs[:, b], hs[:, b], per_row(shift_a, b), ALU.add).then_inc(h_ready, 1)
                if b + 1 < B:
                    power(0, b + 1, 0, STEPS, 2 * b + 2)
                power(1, b, 0, STEPS, 2 * b + 3 if b + 1 < B else 2 * B)
                if b > 0:
                    base(b - 1)
            base(B - 1)
            pool.wait_ge(xz_mm, 8 * B)
            pool.iota(token_of[:, :, :], pattern=[[1, STEPS], [STEPS, CH]], base=0, channel_multiplier=0,
                      allow_small_or_imprecise_dtypes=True).then_inc(const_ready, 1)
            pool.iota(batch_row[:, :, :], pattern=[[0, NG], [L, B]], base=0, channel_multiplier=0,
                      allow_small_or_imprecise_dtypes=True).then_inc(const_ready, 1)
            for n in range(UNITS):
                power(2, n // 2, (n % 2) * HALF, HALF, 2 * B + n + 1)

            pool.wait_ge(slots_ready, 1)
            pool.wait_ge(stored[0], 16 * B)
            pool.wait_ge(stored[1], 16 * B)
            for t in range(NG * B):
                pool.indirect_dma_start(
                    out=picked[:, t // B, t % B, :], out_offset=None, in_=norm_rows,
                    in_offset=bass.IndirectOffsetOnAxis(ap=slot_row[:, t:t + 1], axis=0),
                ).then_inc(picked_in[t // B], 16)
            for g in range(NG):
                pool.wait_ge(hi_ready, g + 1)
                pool.tensor_tensor(rest, value, parts[:, g, 0], ALU.subtract).then_inc(rest_ready, 1)
                pool.wait_ge(mid_ready, g + 1)
                pool.tensor_tensor(rest, rest, parts[:, g, 1], ALU.subtract).then_inc(rest_ready, 1)

        @block.scalar
        def _(act):
            act.wait_ge(in_vec, 16)
            act.activation(cond_s[:, :], cond, ACT.Silu).then_inc(cond_ready, 1)
            for b in range(B):
                act.wait_ge(mod_mm, b + 1)
                act.activation(scale_a[:, b, :], xz_bank[b][:, D:2 * D], ACT.Identity, bias=1.0)
                act.activation(shift_a[:, b, :], xz_bank[b][:, 0:D], ACT.Copy).then_inc(mod_ready, 1)
            act.wait_ge(mod_mm, B + 1)
            act.activation(mod_b[:, 0, :], small_bank[:, 0:B], ACT.Copy)
            act.activation(mod_b[:, 1, :], small_bank[:, B:2 * B], ACT.Identity, bias=1.0
                           ).then_inc(mod_ready, 1)

            def silu_conv(b):
                for m in range(M):
                    act.wait_ge(conv_done, 2 * b + m + 1)
                    act.activation(conv[:, m, b], conv[:, m, b], ACT.Silu).then_inc(silu_done, 1)

            for b in range(B):
                if b > 0:
                    silu_conv(b - 1)
                for hf in range(2):
                    act.wait_ge(tr_done, 2 * b + hf + 1)
                    if b > 1:
                        act.wait_ge(xz_mm, 8 * (b - 1))
                    act.activation(xn_t[:, b % 2, hf * HALF:(hf + 1) * HALF, :], tr_bank[hf][:, :],
                                   ACT.Identity, scale=gamma, bias=beta).then_inc(xnt_ready, 1)
                n = 8 * b
                for hf in range(2):
                    for m in range(M):
                        n += 1
                        act.wait_ge(xz_mm, n)
                        if n == 1:
                            act.wait_ge(const_ready, 8)
                        src = xz_bank[(n - 1) % 4]
                        act.activation(u[:, m, hf * HALF:(hf + 1) * HALF, 1:],
                                       src[:, :].rearrange("p (j c) -> p j c", c=CH), ACT.Copy)
                        act.activation(conv[:, m, b, hf * W:(hf + 1) * W], src[:, :], ACT.Identity,
                                       scale=conv_w[:, CONV_TAPS * m + 3:CONV_TAPS * m + 4],
                                       bias=conv_b[:, m:m + 1]).then_inc(xz_read, 1)
                for hf in range(2):
                    for m in range(M):
                        n += 1
                        act.wait_ge(xz_mm, n)
                        act.activation(gate_z[:, m, b, hf * W:(hf + 1) * W], xz_bank[(n - 1) % 4][:, :],
                                       ACT.Tanh, scale=0.5).then_inc(xz_read, 1)
            act.wait_ge(scan_in, B)
            act.activation(y1[:, :, :], y_bank[:, :], ACT.Copy).then_inc(scan_step, 1)
            silu_conv(B - 1)

            for n in range(2, UNITS + 2):
                k = n - 2
                b, hf = k // 2, k % 2
                act.wait_ge(tr3_done, k + 1)
                if k >= 2:
                    act.wait_ge(router_mm, k - 1)
                act.activation(h2_t[:, hf, :], tr3_bank[:, :], ACT.Identity, scale=mod_b[:, 1, b:b + 1],
                               bias=mod_b[:, 0, b:b + 1]).then_inc(h2_ready, 1)
                act.wait_ge(router_mm, k + 1)
                act.wait_ge(base_ready, B)
                act.activation(routed[:, b, hf * HALF:(hf + 1) * HALF, :],
                               router_bank[:, :].rearrange("p (j c) -> p j c", c=CH), ACT.Silu
                               ).then_inc(routed_ready, 1)
            act.wait_ge(logits_mm, 1)
            act.activation(logits[:, :, 0:HALF].rearrange("p c j -> p j c"),
                           logit_bank[0][:, :].rearrange("p (j c) -> p j c", c=CH), ACT.Copy
                           ).then_inc(logits_ready, 1)
            act.wait_ge(max_ready, 1)
            act.wait_ge(logits_ready, 2)
            act.activation(exps, logits[:, :, :].rearrange("p c j -> p (c j)"), ACT.Exp, bias=neg_max[:, 0:1],
                           accum_out=exp_all[:, 0:1]).then_inc(exp_ready, 1)
            act.wait_ge(top_ready, 1)
            act.activation(e_top[:, :], top[:, :], ACT.Exp, bias=neg_max[:, 0:1],
                           accum_out=exp_top[:, 0:1]).then_inc(exp_ready, 1)

            def chosen_norm(g):
                act.wait_ge(ptr_done, g + 1)
                if g >= 2:
                    act.wait_ge(ffn_mm, G * (g - 1))
                for b in range(B):
                    ins = act.activation(picked_t[:, g % 2, :, b, :],
                                         ptr_bank[:, b * P:(b + 1) * P].rearrange("p (q c) -> p q c", q=G),
                                         ACT.Identity, scale=mod_b[:, 1, b:b + 1], bias=mod_b[:, 0, b:b + 1])
                ins.then_inc(pickt_ready, 1)

            def part(g, i):
                if i == 0:
                    act.wait_ge(value_ready, g + 1)
                    act.activation(parts[:, g, 0], value, ACT.Copy).then_inc(hi_ready, 1)
                elif i == 1:
                    act.wait_ge(rest_ready, 2 * g + 1)
                    act.activation(parts[:, g, 1], rest, ACT.Copy).then_inc(mid_ready, 1)
                else:
                    act.wait_ge(rest_ready, 2 * g + 2)
                    act.activation(parts[:, g, 2], rest, ACT.Copy).then_inc(lo_ready, 1)

            chosen_norm(0)
            for e in range(E):
                g, q = e // G, e % G
                act.wait_ge(ffn_mm, e + 1)
                if e >= 2:
                    act.wait_ge(hidden_ready, e - 1)
                act.activation(silu_g[:, e % 2, :], ffn_bank[e % 2][:, 0:FH * P], ACT.Silu
                               ).then_inc(silu_g_ready, 1)
                if g >= 1 and q >= 1:
                    part(g - 1, q - 1)
                if q == G - 1 and g + 1 < NG:
                    chosen_norm(g + 1)
            for i in range(3):
                part(NG - 1, i)

        @block.tensor
        def _(pe):
            pe.wait_ge(in_wmod, 16)
            for b in range(B):
                pe.wait_ge(cond_rows_ready, b + 1)
                pe.matmul(xz_bank[b][:, 0:3 * D], cond_rows[:, b, :], wmod[:, 0:3 * D], start=True, stop=True)
                pe.matmul(xz_bank[b][:, 3 * D:4 * D], cond_rows[:, b, :], wmod[:, 5 * D:6 * D], start=True,
                          stop=True).then_inc(mod_mm, 1)
            pe.matmul(small_bank[:, 0:B], wmod[:, 3 * D:4 * D], cond_s[:, :], start=True, stop=True)
            pe.matmul(small_bank[:, B:2 * B], wmod[:, 4 * D:5 * D], cond_s[:, :], start=True, stop=True
                      ).then_inc(mod_mm, 1)
            step = 0
            for r in range(3):
                tb = powers[:, r, :]
                for k, n in enumerate((1, 2, 4)):
                    step += 1
                    pe.wait_ge(pow_ready, step)
                    pe.matmul(y_bank[0:S, 0:n * S], plain[:, r, k, :], tb[:, S:(n + 1) * S], start=True,
                              stop=True)
                    pe.matmul(y_bank[0:S, n * S:(n + 1) * S], tb[:, n * S:(n + 1) * S], plain[:, r, k, :],
                              start=True, stop=True).then_inc(pow_mm, 1)
            pe.wait_ge(in_bm, 16)
            pe.wait_ge(in_winx, 16)
            pe.wait_ge(pow_ready, 10)
            for m in range(M):
                ins = pe.matmul(y_bank[0:S, 0:D], bm_t[:, m, :], win_x[:, m, :], start=(m == 0),
                                stop=(m == M - 1))
            ins.then_inc(pow_mm, 1)
            pe.wait_ge(pow_ready, 11)
            pe.matmul(y_bank[:, 0:P], bin_w[:, :], powers[:, 0, 0:P], start=True, stop=True)
            pe.wait_ge(const_ready, 7)
            for r in (1, 2):
                ins = pe.matmul(y_bank[:, r * P:(r + 1) * P], select_last[:, :], powers[:, r, 0:P], start=True,
                                stop=True)
            ins.then_inc(pow_mm, 1)

            pe.wait_ge(in_win, 16)
            for b in range(B):
                for hf in range(2):
                    pe.wait_ge(xn_ready, 2 * b + hf + 1)
                    if b > 0:
                        pe.wait_ge(xnt_ready, 2 * (b - 1) + hf + 1)
                    for k in range(HALF):
                        ins = pe.transpose(tr_bank[hf][:, k * P:(k + 1) * P], xn[:, hf * HALF + k, :],
                                           ident[:, :])
                    ins.then_inc(tr_done, 1)
                n = 8 * b
                for part in range(2):
                    for hf in range(2):
                        pe.wait_ge(xnt_ready, 2 * b + hf + 1)
                        for m in range(M):
                            if n >= 4:
                                pe.wait_ge(xz_read, n - 3)
                            elif n == 0:
                                pe.wait_ge(mod_ready, B + 1)
                                pe.wait_ge(gates_ready, B)
                            pe.matmul(xz_bank[n % 4][:, :], win_t[:, part * INNER + m * P:part * INNER + (m + 1) * P],
                                      xn_t[:, b % 2, hf * HALF:(hf + 1) * HALF, :], start=True, stop=True
                                      ).then_inc(xz_mm, 1)
                            n += 1
                    if part == 0:
                        if b == 0:
                            pe.wait_ge(pow_ready, 12)
                        for i in range(STEPS):
                            ins = pe.matmul(y_bank[:, b * CH:(b + 1) * CH], into_pad[:, PAD - S * i:PAD - S * i + P],
                                            xn_t[:, b % 2, i, :], start=(i == 0), stop=(i == STEPS - 1))
                        ins.then_inc(scan_in, 1)

            pe.wait_ge(scan_step, 1)
            y1v = y1[:, :, :].rearrange("p b (C i) -> p b C i", i=STEPS)
            for i in range(STEPS):
                ins = pe.matmul(small_bank[:, 0:B * 16], last_pad[:, 0, PAD - S * i:PAD - S * i + P],
                                y1v[:, :, :, i], start=(i == 0), stop=(i == STEPS - 1))
            ins.then_inc(scan_mm, 1)
            pe.wait_ge(scan_step, 2)
            y2v = y2[:, :, :].rearrange("p b (g i) -> p b g i", i=STEPS)
            for i in range(STEPS):
                ins = pe.matmul(small_bank[:, 64:64 + 2 * B], last_pad[:, 1, PAD - S * i:PAD - S * i + P],
                                y2v[:, :, :, i], start=(i == 0), stop=(i == STEPS - 1))
            ins.then_inc(scan_mm, 1)
            pe.wait_ge(scan_step, 3)
            pe.matmul(small_bank[0:S, 72:72 + B], ident[:, PAD:P], y3[:, :, 0], start=True, stop=True
                      ).then_inc(scan_mm, 1)
            pe.wait_ge(scan_step, 4)
            pe.matmul(small_bank[:, 76:76 + B], powers[:, 2, S:], carry3[:, :], start=True, stop=True
                      ).then_inc(scan_mm, 1)
            pe.wait_ge(scan_step, 5)
            c2 = small_bank[0:S, 128:128 + 16 * B].rearrange("p (b C) -> p b C", b=B)
            for i in range(STEPS):
                n = 2 if i < STEPS - 1 else 1
                ins = pe.matmul(c2[:, :, i + 1:i + 1 + STEPS * (n - 1) + 1:STEPS], ident[:, S * i:S * (i + 1)],
                                y3[:, :, 0:n], start=True, stop=True)
            ins.then_inc(scan_mm, 1)
            pe.wait_ge(scan_step, 6)
            pe.matmul(small_bank[:, 192:192 + 16 * B], powers[:, 1, S:], carry2[:, :, :].rearrange("p b C -> p (b C)"),
                      start=True, stop=True).then_inc(scan_mm, 1)
            pe.wait_ge(scan_step, 7)
            c1 = tr_bank[0][0:S, :].rearrange("p (b C) -> p b C", b=B)
            for i in range(STEPS):
                n = 16 if i < STEPS - 1 else 15
                ins = pe.matmul(c1[:, :, i + 1:i + 1 + STEPS * (n - 1) + 1:STEPS], ident[:, S * i:S * (i + 1)],
                                y2[:, :, 0:n], start=True, stop=True)
            ins.then_inc(scan_mm, 1)
            pe.wait_ge(scan_step, 8)
            pe.matmul(tr_bank[1][:, :], powers[:, 0, S:], carry1[:, :, :].rearrange("p b C -> p (b C)"),
                      start=True, stop=True).then_inc(scan_mm, 1)

            pe.wait_ge(in_c, 16 * STEPS)
            pe.wait_ge(xz_read, 8 * B)
            for n in range(UNITS + 2):
                if n < UNITS:
                    b, hf = n // 2, n % 2
                    if n == 0:
                        pe.wait_ge(state_ready, 1)
                    else:
                        pe.wait_ge(sc_read, 2 * n)
                    for m in range(M):
                        for k in range(HALF):
                            ins = pe.matmul(sc_bank[m][:, k * CH:(k + 1) * CH],
                                            c_block[:, hf * HALF + k, m * P:(m + 1) * P], y1[:, b, :],
                                            start=True, stop=True)
                        ins.then_inc(sc_mm, 1)
                if n >= 2:
                    k2 = n - 2
                    pe.wait_ge(xhat3_ready, k2 + 1)
                    if k2 >= 1:
                        pe.wait_ge(h2_ready, k2)
                    for k in range(HALF):
                        ins = pe.transpose(tr3_bank[:, k * P:(k + 1) * P], xhat3[:, k2 % 2, k, :], ident[:, :])
                    ins.then_inc(tr3_done, 1)
                if 1 <= n <= UNITS:
                    k1 = n - 1
                    b = k1 // 2
                    pe.wait_ge(y_ready, 2 * (k1 + 1))
                    pe.wait_ge(wout_ready, B)
                    if k1 >= 1:
                        pe.wait_ge(x1_ready, k1)
                    for k in range(HALF):
                        for m in range(M):
                            ins = pe.matmul(out_bank[:, k * D:(k + 1) * D], y[:, k1 % 2, m, k * P:(k + 1) * P],
                                            wout_g[:, b, m, :], start=(m == 0), stop=(m == M - 1))
                    ins.then_inc(out_mm, 1)
                if n >= 2:
                    k2 = n - 2
                    pe.wait_ge(h2_ready, k2 + 1)
                    pe.wait_ge(in_r1, 16)
                    if k2 >= 1:
                        pe.wait_ge(routed_ready, k2)
                    pe.matmul(router_bank[:, :], r1[:, :], h2_t[:, k2 % 2, :], start=True, stop=True
                              ).then_inc(router_mm, 1)
            pe.wait_ge(in_r2, 16)
            pe.wait_ge(routed_ready, UNITS)
            for hf in range(2):
                for b in range(B):
                    ins = pe.matmul(logit_bank[hf][32 * b:32 * b + 32, :], r2[:, :],
                                    routed[:, b, hf * HALF:(hf + 1) * HALF, :], start=True, stop=True)
                ins.then_inc(logits_mm, 1)
            pick = ident[:, :].rearrange("p (b r q) -> p q r b", b=B, q=G)
            for what, (src, ready) in enumerate(((top_at_f, 1), (w_top, 2))):
                pe.wait_ge(weights_ready, ready)
                for q in range(G):
                    ins = pe.matmul(slot_bank[what][32 * q:32 * q + 32, 0:NG * B], src[:, :],
                                    pick[:, q, 0:NG, :], start=True, stop=True)
                ins.then_inc(slots_mm, 1)

            def pick_transposes(g):
                pe.wait_ge(picked_in[g], 16 * B)
                if g >= 1:
                    pe.wait_ge(pickt_ready, g)
                for b in range(B):
                    ins = pe.transpose(ptr_bank[:, b * P:(b + 1) * P], picked[:, g, b, :], ident[:, :])
                ins.then_inc(ptr_done, 1)

            def expert_out(g):
                pe.wait_ge(hidden_ready, G * (g + 1))
                if g >= 1:
                    pe.wait_ge(value_ready, g)
                for b in range(B):
                    for f in range(FH):
                        for q in range(G):
                            s = (g * G + q) % SLOTS
                            w3_s = experts[:, s, 2 * DFF + f * D:2 * DFF + (f + 1) * D]
                            ins = pe.matmul(eout_bank[32 * q:32 * q + 32, b * D:(b + 1) * D],
                                            hidden[:, q, f, b * CAPACITY:(b + 1) * CAPACITY], w3_s,
                                            start=(f == 0), stop=(f == FH - 1))
                ins.then_inc(eout_mm, 1)

            pick_transposes(0)
            for e in range(E):
                g, q, s = e // G, e % G, e % SLOTS
                pe.wait_ge(in_expert[s], 48 * (e // SLOTS + 1))
                pe.wait_ge(pickt_ready, g + 1)
                if e >= 2:
                    pe.wait_ge(hidden_ready, e - 1)
                for half in range(2):
                    for f in range(FH):
                        at = half * DFF + f * P
                        ins = pe.matmul(ffn_bank[e % 2][:, (half * FH + f) * P:(half * FH + f + 1) * P],
                                        experts[:, s, at:at + P], picked_t[:, g % 2, q], start=True,
                                        stop=True)
                ins.then_inc(ffn_mm, 1)
                if q == 0 and g >= 1:
                    expert_out(g - 1)
                if q == 2 and g + 1 < NG:
                    pick_transposes(g + 1)
            expert_out(NG - 1)

            pe.wait_ge(onehot_ready, NG * B)
            pe.wait_ge(lo_ready, NG)
            for n in range(UNITS):
                b, hf = n // 2, n % 2
                if n >= 3:
                    pe.wait_ge(final_ready, n - 2)
                for k in range(HALF):
                    j = hf * HALF + k
                    for g in range(NG):
                        for part in range(3):
                            ins = pe.matmul(scatter_bank[n % 3][:, k * D:(k + 1) * D],
                                            onehot[:, g, b, j * CH:(j + 1) * CH], parts[:, g, part, b, :],
                                            start=(g == 0 and part == 0), stop=(g == NG - 1 and part == 2))
                ins.then_inc(scatter_mm, 1)

        @block.vector
        def _(dve):
            order = Order(dve, dve_order)
            dve.memset(ones[:, :], 1.0).then_inc(ones_ready, 1)

            def ln_stats(kind, src, stats, b, j0, n):
                for j in range(n):
                    ins = dve.bn_stats(stats[:, j, :], src(j))
                order.after(ins)
                mu_e, mu_o = stats[:, 0:n, 1], stats[:, 0:n, 4]
                m2_e, m2_o = stats[:, 0:n, 2], stats[:, 0:n, 5]
                total, gap, m2, gap2 = (tmp[:, k, 0:n] for k in range(4))
                dve.tensor_tensor(gap, mu_e, mu_o, ALU.subtract)
                dve.tensor_tensor(total, mu_e, mu_o, ALU.add)
                order.after(dve.tensor_tensor(m2, m2_e, m2_o, ALU.add))
                dve.tensor_scalar(mean[:, kind, b, j0:j0 + n], total, 0.5, None, ALU.mult)
                dve.tensor_scalar(m2, m2, 1.0 / D, LN_EPS, ALU.mult, ALU.add)
                order.after(dve.tensor_tensor(gap2, gap, gap, ALU.mult))
                dve.scalar_tensor_tensor(out=var[:, kind, b, j0:j0 + n], in0=gap2, scalar=0.25, in1=m2,
                                         op0=ALU.mult, op1=ALU.add).then_inc(var_ready, 1)

            def normalise(kind, dst, src, b, j0, n):
                for j in range(n):
                    ins = dve.tensor_scalar(dst(j), src(j), mean[:, kind, b, j0 + j:j0 + j + 1],
                                            rstd[:, kind, b, j0 + j:j0 + j + 1], ALU.subtract, ALU.mult)
                return ins

            def stats_a(b):
                dve.wait_ge(in_x[b], 16)
                ln_stats(0, lambda j: xs[:, b, j, :], st1, b, 0, STEPS)

            def conv_taps(b, m):
                if m == 0:
                    dve.wait_ge(xz_read, 8 * b + 4)
                acc = conv[:, m, b].rearrange("p (j c) -> p j c", c=CH)
                for s in range(1, CONV_TAPS):
                    w = conv_w[:, CONV_TAPS * m + 3 - s:CONV_TAPS * m + 4 - s]
                    dve.scalar_tensor_tensor(out=acc[:, s:, :], in0=u[:, m, 0:STEPS - s, 1:], scalar=w,
                                             in1=acc[:, s:, :], op0=ALU.mult, op1=ALU.add)
                    ins = dve.scalar_tensor_tensor(out=acc[:, 0:s, :], in0=u[:, m, STEPS - s:, 0:CH], scalar=w,
                                                   in1=acc[:, 0:s, :], op0=ALU.mult, op1=ALU.add)
                    if s < CONV_TAPS - 1:
                        order.after(ins)
                ins.then_inc(conv_done, 1)

            stats_a(0)
            dve.wait_ge(ones_ready, 1)
            dve.wait_ge(cond_ready, 1)
            for b in range(B):
                dve.tensor_scalar(cond_rows[:, b, :], ones[:, :], cond_s[:, b:b + 1], None, ALU.mult
                                  ).then_inc(cond_rows_ready, 1)
            for b in range(B):
                dve.wait_ge(mod_ready, b + 1)
                raw = xz_bank[b][:, 2 * D:4 * D]
                if b > 0:
                    dve.wait_ge(gates_ready, b)
                order.after(dve.tensor_scalar(gate_sign, raw, 0.0, 2.0, ALU.is_ge, ALU.mult))
                order.after(dve.scalar_tensor_tensor(out=gate_size, in0=gate_sign, scalar=-1.0, in1=raw,
                                                     op0=ALU.add, op1=ALU.mult))
                order.after(dve.tensor_scalar(gate_size, gate_size, 0.25, None, ALU.max))
                dve.scalar_tensor_tensor(out=gates[:, b, :], in0=gate_sign, scalar=-1.0,
                                         in1=gate_size, op0=ALU.add, op1=ALU.mult).then_inc(gates_ready, 1)
            dve.wait_ge(const_ready, 1)
            dve.wait_ge(in_a, 16)
            for r in range(3):
                dve.tensor_copy(powers[:, r, 0:S], ident[0:S, 0:S])
            dve.tensor_copy(powers[:, 0, S:2 * S], apair[:, 1, :])
            dve.tensor_copy(plain[:, 0, 0, :], apair[:, 0, :]).then_inc(pow_ready, 1)
            step = 0
            for r in range(3):
                for k, n in enumerate((1, 2, 4)):
                    step += 1
                    dve.wait_ge(pow_mm, step)
                    ins = dve.tensor_copy(powers[:, r, (n + 1) * S:(2 * n + 1) * S], y_bank[0:S, 0:n * S])
                    if n == 4 and r < 2:
                        dve.tensor_copy(powers[:, r + 1, S:2 * S], y_bank[0:S, 3 * S:4 * S])
                        ins = dve.tensor_copy(plain[:, r + 1, 0, :], y_bank[0:S, 4 * S:5 * S])
                    elif n < 4:
                        ins = dve.tensor_copy(plain[:, r, k + 1, :], y_bank[0:S, n * S:(n + 1) * S])
                    ins.then_inc(pow_ready, 1)
            dve.wait_ge(pow_mm, 10)
            dve.tensor_copy(bin_w[:, :], y_bank[0:S, 0:D]).then_inc(pow_ready, 1)
            dve.wait_ge(pow_mm, 11)
            dve.wait_ge(const_ready, 6)
            dve.tensor_copy(into_pad[:, PAD:], y_bank[:, 0:P])
            dve.tensor_copy(last_pad[:, 0, PAD:], y_bank[:, P:2 * P])
            dve.tensor_copy(last_pad[:, 1, PAD:], y_bank[:, 2 * P:3 * P]).then_inc(pow_ready, 1)

            for b in range(B):
                if b > 0:
                    dve.wait_ge(h_ready, b)
                dve.wait_ge(rstd_ready, 1 if b == 0 else 2 * b)
                normalise(0, lambda j: xhat[:, j, :], lambda j: xs[:, b, j, :], b, 0, STEPS
                          ).then_inc(xhat_ready, 1)
                if b + 1 < B:
                    stats_a(b + 1)
                if b > 0:
                    conv_taps(b - 1, 0)
                dve.wait_ge(h_ready, b + 1)
                ln_stats(1, lambda j: hs[:, b, j, :], st2, b, 0, STEPS)
                if b > 0:
                    conv_taps(b - 1, 1)
                    dve.wait_ge(tr_done, 2 * b)
                dve.wait_ge(rstd_ready, 2 * b + 3 if b + 1 < B else 2 * B)
                for hf in range(2):
                    normalise(1, lambda j: xn[:, hf * HALF + j, :], lambda j: hs[:, b, hf * HALF + j, :], b,
                              hf * HALF, HALF).then_inc(xn_ready, 1)
            dve.wait_ge(in_wout, 16)
            for b in range(B):
                for m in range(M):
                    ins = dve.scalar_tensor_tensor(out=wout_g[:, b, m, :], in0=wout_t[:, m, :], scalar=0.5,
                                                   in1=gates[:, b, 0:D], op0=ALU.mult, op1=ALU.mult)
                ins.then_inc(wout_ready, 1)

            dve.wait_ge(scan_mm, 1)
            dve.tensor_copy(y2[:, :, :].rearrange("p b C -> p (b C)"), small_bank[:, 0:16 * B]).then_inc(scan_step, 1)
            dve.wait_ge(scan_mm, 2)
            dve.tensor_copy(y3[:, :, :].rearrange("p b C -> p (b C)"), small_bank[:, 64:64 + 2 * B]
                            ).then_inc(scan_step, 1)
            dve.wait_ge(scan_mm, 3)
            dve.tensor_copy(carry3[:, :], small_bank[0:S, 72:72 + B]).then_inc(scan_step, 1)
            dve.wait_ge(scan_mm, 4)
            dve.tensor_tensor(y3[:, :, 1], y3[:, :, 1], small_bank[:, 76:76 + B], ALU.add).then_inc(scan_step, 1)
            dve.wait_ge(scan_mm, 5)
            dve.wait_ge(const_ready, 10)
            dve.tensor_copy(carry2[:, :, 1:], small_bank[0:S, 128:128 + 16 * B].rearrange(
                "p (b C) -> p b C", b=B)[:, :, 1:]).then_inc(scan_step, 1)
            dve.wait_ge(scan_mm, 6)
            dve.tensor_tensor(y2[:, :, :].rearrange("p b C -> p (b C)"), y2[:, :, :].rearrange("p b C -> p (b C)"),
                              small_bank[:, 192:192 + 16 * B], ALU.add).then_inc(scan_step, 1)
            dve.wait_ge(scan_mm, 7)
            dve.tensor_copy(carry1[:, :, 1:], tr_bank[0][0:S, :].rearrange("p (b C) -> p b C", b=B)[:, :, 1:]
                            ).then_inc(scan_step, 1)
            dve.wait_ge(scan_mm, 8)
            dve.tensor_tensor(y1[:, :, :].rearrange("p b C -> p (b C)"), y1[:, :, :].rearrange("p b C -> p (b C)"),
                              tr_bank[1][:, :], ALU.add).then_inc(state_ready, 1)
            conv_taps(B - 1, 0)
            conv_taps(B - 1, 1)

            for n in range(UNITS + 2):
                if n < UNITS:
                    b, hf = n // 2, n % 2
                    cols = slice(hf * W, (hf + 1) * W)
                    dve.wait_ge(silu_done, 2 * (b + 1))
                    if n >= 2:
                        dve.wait_ge(out_mm, n - 1)
                    for m in range(M):
                        dve.wait_ge(sc_mm, 2 * n + m + 1)
                        dve.tensor_tensor(conv[:, m, b, cols], conv[:, m, b, cols], sc_bank[m][:, :],
                                          ALU.add).then_inc(sc_read, 1)
                        dve.wait_ge(sc_read, 2 * n + m + 1)
                        dve.scalar_tensor_tensor(out=y[:, n % 2, m, :], in0=gate_z[:, m, b, cols], scalar=1.0,
                                                 in1=conv[:, m, b, cols], op0=ALU.add, op1=ALU.mult
                                                 ).then_inc(y_ready, 1)
                if n >= 2:
                    k2 = n - 2
                    b, hf = k2 // 2, k2 % 2
                    dve.wait_ge(rstd_ready, 2 * B + k2 + 1)
                    if k2 >= 2:
                        dve.wait_ge(tr3_done, k2 - 1)
                        dve.wait_ge(stored[hf], 16 * (k2 // 2))
                    normalise(2, lambda j: xhat3[:, hf, j, :], lambda j: hs[:, b, hf * HALF + j, :], b,
                              hf * HALF, HALF).then_inc(xhat3_ready, 1)
                if 1 <= n <= UNITS:
                    k1 = n - 1
                    b, hf = k1 // 2, k1 % 2
                    dve.wait_ge(out_mm, k1 + 1)
                    dve.wait_ge(base_ready, b + 1)
                    rows = hs[:, b, hf * HALF:(hf + 1) * HALF, :].rearrange("p j d -> p (j d)")
                    dve.tensor_tensor(rows, rows, out_bank[:, :], ALU.add).then_inc(x1_ready, 1)
                    dve.wait_ge(x1_ready, k1 + 1)
                    ln_stats(2, lambda j: hs[:, b, hf * HALF + j, :], st1, b, hf * HALF, HALF)

            dve.wait_ge(logits_mm, 2)
            dve.tensor_copy(logits[:, :, HALF:].rearrange("p c j -> p j c"),
                            logit_bank[1][:, :].rearrange("p (j c) -> p j c", c=CH)).then_inc(logits_ready, 1)
            dve.wait_ge(logits_ready, 2)
            flat = logits[:, :, :].rearrange("p c j -> p (c j)")
            for r in range(CAPACITY // 8):
                src = flat if r == 0 else left
                eight = top[:, 8 * r:8 * r + 8]
                order.after(dve.max(eight, src))
                if r == 0:
                    dve.tensor_scalar(neg_max[:, :], top[:, 0:1], -1.0, None, ALU.mult).then_inc(max_ready, 1)
                ins = dve.max_index(top_at[:, 8 * r:8 * r + 8], eight, src)
                if r + 1 < CAPACITY // 8:
                    order.after(dve.match_replace(left, eight, src, LOWEST))
                else:
                    ins.then_inc(top_ready, 1)
            dve.wait_ge(top_ready, 1)
            dve.tensor_copy(top_at_f[:, :], top_at[:, :]).then_inc(weights_ready, 1)
            dve.wait_ge(exp_ready, 2)
            order.after(dve.reciprocal(rz[:, :], exp_all[:, :]))
            order.after(dve.tensor_scalar(den[:, :], exp_top[:, :], rz[:, 0:1], 1e-9, ALU.mult, ALU.add))
            order.after(dve.reciprocal(rden[:, :], den[:, :]))
            dve.tensor_scalar(w_top[:, :], e_top[:, :], rz[:, 0:1], rden[:, 0:1], ALU.mult, ALU.mult
                              ).then_inc(weights_ready, 1)
            dve.wait_ge(slots_mm, 1)
            dve.wait_ge(const_ready, 12)
            dve.tensor_copy(slot_at[:, 0, :], slot_bank[0][:, 0:NG * B])
            dve.tensor_tensor(slot_row[:, :], slot_bank[0][:, 0:NG * B], batch_row[:, :, :].rearrange("p g b -> p (g b)"),
                              ALU.add).then_inc(slots_ready, 1)
            dve.wait_ge(slots_mm, 2)
            dve.tensor_copy(slot_at[:, 1, :], slot_bank[1][:, 0:NG * B]).then_inc(slots_ready, 1)
            dve.wait_ge(slots_ready, 2)

            def one_hot(t):
                dve.tensor_scalar(onehot[:, t // B, t % B, :], token_of[:, :, :].rearrange("p j c -> p (j c)"),
                                  slot_at[:, 0, t:t + 1], None, ALU.is_equal).then_inc(onehot_ready, 1)

            def expert_value(g):
                dve.wait_ge(eout_mm, g + 1)
                if g >= 1:
                    dve.wait_ge(lo_ready, g)
                for b in range(B):
                    ins = dve.scalar_tensor_tensor(out=value[:, b, :], in0=eout_bank[:, b * D:(b + 1) * D],
                                                   scalar=slot_at[:, 1, g * B + b:g * B + b + 1],
                                                   in1=gates[:, b, D:2 * D], op0=ALU.mult, op1=ALU.mult)
                ins.then_inc(value_ready, 1)

            for e in range(E):
                g, q = e // G, e % G
                one_hot(e)
                dve.wait_ge(silu_g_ready, e + 1)
                if e >= G and q == 0:
                    dve.wait_ge(eout_mm, g)
                dve.tensor_tensor(hidden[:, q].rearrange("p f t -> p (f t)"), silu_g[:, e % 2, :],
                                  ffn_bank[e % 2][:, FH * P:2 * FH * P], ALU.mult).then_inc(hidden_ready, 1)
                if g >= 1 and q == 1:
                    expert_value(g - 1)
            expert_value(NG - 1)
            for n in range(UNITS):
                b, hf = n // 2, n % 2
                dve.wait_ge(scatter_mm, n + 1)
                rows = hs[:, b, hf * HALF:(hf + 1) * HALF, :].rearrange("p j d -> p (j d)")
                dve.tensor_tensor(rows, rows, scatter_bank[n % 3][:, :], ALU.add).then_inc(final_ready, 1)


def kernel(**inputs):
    import numpy as np
    import concourse.bacc as bacc
    from concourse.bass_utils import run_bass_kernel_spmd

    a = {n: np.ascontiguousarray(v) for n, v in inputs.items()}
    t = np.ascontiguousarray
    d = a["L0_attn_x"].shape[-1]
    inner = a["L0_attn_conv_w"].shape[0]
    m = inner // d
    vectors = np.concatenate([
        a["L0_c"].T, a["L0_attn_ln_gamma"][:, None], a["L0_attn_ln_beta"][:, None],
        a["L0_attn_conv_b"].reshape(m, d).T,
        a["L0_attn_conv_w"].reshape(m, d, -1).transpose(1, 0, 2).reshape(d, -1)], axis=1)
    arrays = dict(
        x=a["L0_attn_x"], vectors=t(vectors), w_mod=a["L0_wmod"],
        w_in_t=t(a["L0_attn_W_in"].T),
        w_in_x=t(a["L0_attn_W_in"][:inner].reshape(m, d, d).transpose(1, 0, 2)),
        w_out_t=t(a["L0_attn_W_out"].T.reshape(m, d, d).transpose(1, 0, 2)),
        a_pair=t(np.stack([a["L0_attn_A"], a["L0_attn_A"].T], axis=1)),
        c_m=a["L0_attn_Cm"],
        b_m_t=t(a["L0_attn_Bm"].T.reshape(m, d, -1).transpose(1, 0, 2)),
        router_w1=a["L0_ffn_router_w1"], router_w2=a["L0_ffn_router_w2"],
        w1=a["L0_ffn_w1"], w2=a["L0_ffn_w2"],
        w3=t(a["L0_ffn_w3"].reshape(a["L0_ffn_w3"].shape[0], -1, d, d).transpose(0, 2, 1, 3)),
    )
    nc = bacc.Bacc("TRN2", target_bir_lowering=False, num_devices=1)
    args = {n: nc.dram_tensor(f"in_{n}", v.shape, mybir.dt.from_np(v.dtype), kind="ExternalInput").ap()
            for n, v in arrays.items()}
    out = nc.dram_tensor("out_0", arrays["x"].shape, F32, kind="ExternalOutput").ap()
    adaln_block(nc, out=out, **args)
    r = run_bass_kernel_spmd(nc, [{f"in_{n}": v for n, v in arrays.items()}], core_ids=[0])
    return r.results[0]["out_0"]
```

```python
from contextlib import ExitStack

import concourse.bass as bass
from concourse import mybir

F32 = mybir.dt.float32
BF16 = mybir.dt.bfloat16
U32 = mybir.dt.uint32
I32 = mybir.dt.int32
ALU = mybir.AluOpType
ACT = mybir.ActivationFunctionType

P = 128
STEPS = 8
LN_EPS = 1e-5
CAPACITY = 32
CONV_TAPS = 4
LOWEST = -3.4028234e38


class Order:

    def __init__(self, eng, sem):
        self.eng, self.sem, self.at = eng, sem, 0

    def after(self, ins):
        self.at += 1
        ins.then_inc(self.sem, 1)
        self.eng.wait_ge(self.sem, self.at)


def adaln_block(nc, x, vectors, w_mod, w_in_t, w_in_x, w_out_t, a_pair, c_m, b_m_t, router_w1,
                router_w2, w1, w2, w3, out):
    B, L, D = x.shape
    CH = L // STEPS
    INNER = w_in_t.shape[1] // 2
    M = INNER // P
    S = a_pair.shape[0]
    E, _, DFF = w1.shape
    FH = DFF // P
    G = 4
    NG = E // G
    HALF = STEPS // 2
    W = HALF * CH
    UNITS = 2 * B
    FFN_BUFS = 3
    SLOTS = 8
    PAD = (STEPS - 1) * S
    assert CH == P and D == P and M == 2 and STEPS * S == P and G * CAPACITY == P and W == 512
    assert B == 4 and CH == 2 * STEPS * STEPS and E <= 32

    x_rows = x.rearrange("b (c j) d -> b c (j d)", j=STEPS)
    out_rows = out.rearrange("b (c j) d -> b c (j d)", j=STEPS)
    norm_rows = nc.dram_tensor("norm_rows", [B * L, D], F32, kind="Internal").ap()
    norm_by_chunk = norm_rows.rearrange("(b c j) d -> b c (j d)", b=B, j=STEPS)

    with ExitStack() as ctx:
        def sb(name, shape, dt=F32):
            return ctx.enter_context(nc.sbuf_tensor(name, shape, dt))

        def sem(name):
            return ctx.enter_context(nc.semaphore(name))

        bank = [ctx.enter_context(nc.psum_tensor(f"bank{i}", [P, W], F32)) for i in range(8)]

        ident = sb("ident", [P, P])
        ones = sb("ones", [P, P])
        minus_half = sb("minus_half", [P, STEPS])
        batch_row = sb("batch_row", [P, NG, B])
        select_last = sb("select_last", [S, P])
        vec = sb("vec", [P, vectors.shape[1]])
        cond = vec[:, 0:4]
        gamma, beta = vec[:, 4:5], vec[:, 5:6]
        conv_b = vec[:, 6:8]
        conv_w = vec[:, 8:16]
        win_t = sb("win_t", [P, 2 * INNER])
        win_x = sb("win_x", [P, M, D])
        wout_t = sb("wout_t", [P, M, D])
        apair = sb("apair", [S, 2, S])
        bm_t = sb("bm_t", [P, M, S])
        c_block = sb("c_block", [P, STEPS, INNER])
        r1 = sb("r1", [P, P])
        r2 = sb("r2", [P, 2, 2 * E])
        next_half = sb("next_half", [P, P])
        lane = sb("lane", [P, 1], I32)
        half_start = sb("half_start", [P, 1])
        experts = sb("experts", [P, SLOTS, 2 * DFF + FH * D])

        cond_s = sb("cond_s", [P, B])
        shift_a = sb("shift_a", [P, B, D])
        scale_a = sb("scale_a", [P, B, D])
        gates = sb("gates", [P, B, 2 * D])
        mod_b = sb("mod_b", [P, 2, B])
        wout_g = sb("wout_g", [P, B, M, D])

        powers = sb("powers", [S, 3, (STEPS + 1) * S])
        plain = sb("plain", [S, 3, 4, S])
        bin_w = sb("bin_w", [S, D])
        into_pad = sb("into_pad", [P, PAD + P])
        last_pad = sb("last_pad", [P, 2, PAD + P])
        y1 = sb("y1", [P, B, CH])
        y2 = sb("y2", [P, B, 16])
        y3 = sb("y3", [P, B, 2])
        carry3 = sb("carry3", [S, B])
        carry2 = sb("carry2", [S, B, 16])
        carry1 = sb("carry1", [S, B, CH])

        xs = sb("xs", [P, B, STEPS, D])
        hs = sb("hs", [P, B, STEPS, D])
        xhat = sb("xhat", [P, STEPS, D])
        xn = sb("xn", [P, STEPS, D])
        xn_t = sb("xn_t", [P, 2, STEPS, CH])
        HALO = CONV_TAPS - 1
        u = sb("u", [P, M, HALO + STEPS, CH])
        conv = sb("conv", [P, M, B, STEPS * CH])
        gate_z = sb("gate_z", [P, M, B, STEPS * CH])
        y = sb("y", [P, 2, M, W])
        early = y[:, :, :, :].rearrange("p a m t -> p (a m t)")
        wmod = early[:, 0:6 * D]
        cond_rows = early[:, 6 * D:(6 + B) * D].rearrange("p (b t) -> p b t", b=B)
        gate_a_parts = gate_z[:, 0, B - 1].rearrange("p (a b t) -> p a b t", a=2, b=B)
        gate_b_parts = y[:, 0].rearrange("p a (b t) -> p a b t", b=B)
        token_of = xn_t[:, 0]
        xhat3 = sb("xhat3", [P, 2, HALF, D])
        h2_t = sb("h2_t", [P, 2, W])
        routed = xs
        st1 = sb("st1", [P, STEPS, 6])
        st2 = sb("st2", [P, STEPS, 6])
        mean_var = sb("mean_var", [P, STEPS, 2])
        neg_mean = sb("neg_mean", [P, 3, B, STEPS])
        neg_shift = sb("neg_shift", [P, 3, B, STEPS])
        var = sb("var", [P, 3, B, STEPS])
        rstd = sb("rstd", [P, 3, B, STEPS])

        CH2 = CH // 2
        left = [xn[:, k * HALF:(k + 1) * HALF, :].rearrange("p j d -> p (j d)") for k in range(2)]
        exps = xhat[:, 0:HALF, :].rearrange("p j d -> p (j d)")
        found = sb("found", [P, 2 * CAPACITY])
        found_at = sb("found_at", [P, CAPACITY], U32)
        neg_max = sb("neg_max", [P, 2])
        half_max = sb("half_max", [P, 2])
        half_sum = sb("half_sum", [P, 2])
        half_part = sb("half_part", [P, 2])
        best = sb("best", [P, CAPACITY])
        best_token = sb("best_token", [P, CAPACITY])
        keep = sb("keep", [P, CAPACITY])
        exp_all = sb("exp_all", [P, 2])
        exp_top = sb("exp_top", [P, 1])
        e_top = sb("e_top", [P, CAPACITY])
        rz = sb("rz", [P, 1])
        den = sb("den", [P, 1])
        rden = sb("rden", [P, 1])
        w_top = sb("w_top", [P, CAPACITY])
        slot_at = sb("slot_at", [P, 2, NG * B])
        slot_row = sb("slot_row", [P, NG * B], U32)

        def over(base, at, dt, *shape):
            n = 1
            for d in shape:
                n *= d
            flat = base[:, :, :, :].rearrange("p m b t -> p (m b t)")
            size = 2 if dt == BF16 else 4
            ap = flat[:, at // 4:(at + n * size) // 4]
            ap = ap if dt == F32 else ap.bitcast(dt)
            names = "abcdef"[:len(shape)]
            return ap.rearrange(f"p ({' '.join(names)}) -> p {' '.join(names)}",
                                **dict(zip(names[1:], shape[1:]))), at + n * size

        onehot, _ = over(conv, 0, BF16, NG, B, STEPS * CH)
        picked, at = over(gate_z, 0, F32, NG, B, D)
        picked_t, at = over(gate_z, at, F32, 2, G, B, CAPACITY)
        silu_g, at = over(gate_z, at, F32, FFN_BUFS, FH * P)
        hidden = xn_t[:, 1].rearrange("p (q f) t -> p q f t", q=G)
        value, at = over(gate_z, at, F32, B, D)
        rest, at = over(gate_z, at, F32, B, D)
        parts, at = over(gate_z, at, BF16, NG, 3, B, D)

        in_x = [sem(f"in_x{b}") for b in range(B)]
        in_x0_rest = sem("in_x0_rest")
        in_vec, in_wmod, in_win, in_winx, in_wout, in_a, in_bm = (
            sem(n) for n in ("in_vec", "in_wmod", "in_win", "in_winx", "in_wout", "in_a", "in_bm"))
        in_c, in_r1, in_r2 = sem("in_c"), sem("in_r1"), sem("in_r2")
        in_expert = [sem(f"in_expert{i}") for i in range(SLOTS)]
        in_expert_out = [sem(f"in_expert_out{i}") for i in range(SLOTS)]
        const_ready = sem("const_ready")
        pool_order, dve_order, act_order = sem("pool_order"), sem("dve_order"), sem("act_order")
        ones_ready = sem("ones_ready")
        cond_ready = sem("cond_ready")
        cond_rows_ready = sem("cond_rows_ready")
        mod_mm = sem("mod_mm")
        mod_ready = sem("mod_ready")
        raw_ready = sem("raw_ready")
        gates_ready = sem("gates_ready")
        wout_ready = sem("wout_ready")
        pow_mm, pow_ready = sem("pow_mm"), sem("pow_ready")
        var_ready, rstd_ready = sem("var_ready"), sem("rstd_ready")
        moments_ready = sem("moments_ready")
        xhat_ready, h_ready, xn_ready = sem("xhat_ready"), sem("h_ready"), sem("xn_ready")
        h0_ready = sem("h0_ready")
        base_ready = sem("base_ready")
        tr_done, xnt_ready = sem("tr_done"), sem("xnt_ready")
        xz_mm, u_ready, xz_read = sem("xz_mm"), sem("u_ready"), sem("xz_read")
        scan_in = sem("scan_in")
        tap_done, conv_done, silu_done = sem("tap_done"), sem("conv_done"), sem("silu_done")
        scan_mm, scan_step = sem("scan_mm"), sem("scan_step")
        state_ready = sem("state_ready")
        sc_mm, sc_read, y_ready = sem("sc_mm"), sem("sc_read"), sem("y_ready")
        out_mm, x1_ready = sem("out_mm"), sem("x1_ready")
        xhat3_ready, stored = sem("xhat3_ready"), [sem("stored0"), sem("stored1")]
        tr3_done, h2_ready, router_mm, routed_ready = (
            sem("tr3_done"), sem("h2_ready"), sem("router_mm"), sem("routed_ready"))
        logits_mm, logits_ready = sem("logits_mm"), sem("logits_ready")
        left_ready, index_ready = sem("left_ready"), sem("index_ready")
        found_ready, other_mm, merged = sem("found_ready"), sem("other_mm"), sem("merged")
        max_ready, exp_ready, top_ready, weights_ready = (
            sem("max_ready"), sem("exp_ready"), sem("top_ready"), sem("weights_ready"))
        slots_mm, slots_ready = sem("slots_mm"), sem("slots_ready")
        picked_in = [sem(f"picked_in{g}") for g in range(NG)]
        ptr_done, pickt_ready = sem("ptr_done"), sem("pickt_ready")
        ffn_mm, silu_g_ready, hidden_ready = sem("ffn_mm"), sem("silu_g_ready"), sem("hidden_ready")
        eout_mm, value_ready = sem("eout_mm"), sem("value_ready")
        hi_ready, mid_ready, lo_ready, rest_ready = (
            sem("hi_ready"), sem("mid_ready"), sem("lo_ready"), sem("rest_ready"))
        onehot_ready = sem("onehot_ready")
        scatter_mm, final_ready = sem("scatter_mm"), sem("final_ready")
        out_stored = sem("out_stored")

        tr_bank = bank[0:2]
        xz_bank = bank[2:6]
        y_bank, small_bank = bank[6], bank[7]
        sc_bank, out_bank, tr3_bank, router_bank = bank[2:4], bank[4], (bank[0], bank[7]), (bank[1], bank[6])
        logit_bank, other_bank = bank[5], bank[6]
        ptr_bank, slot_bank, ffn_bank, eout_bank = bank[0], (bank[1], bank[7]), bank[1:4], bank[4]
        scatter_bank = bank[5:8] + bank[1:4] + [bank[0], bank[4]]

        VAR1 = [1, 2] + [b + 2 for b in range(2, B)]
        VAR2 = [3] + [B + b + 1 for b in range(1, B)]

        H_READY = [[1, None]] + [[2 * b, 2 * b + 1] for b in range(1, B)]

        POW = (0, 5, 8)

        block = ctx.enter_context(nc.Block())

        @block.sync
        def _(sp):
            sp.dma_start(vec[:, :], vectors).then_inc(in_vec, 16)
            for hf in range(2):
                sp.dma_start(xs[:, 0, hf * HALF:(hf + 1) * HALF].rearrange("p j d -> p (j d)"),
                             x_rows[0][:, hf * W:(hf + 1) * W]).then_inc(in_x[0] if hf == 0 else in_x0_rest, 16)
            sp.dma_start(wmod[:, :], w_mod).then_inc(in_wmod, 16)
            sp.dma_start(apair[:, :, :], a_pair).then_inc(in_a, 16)
            sp.dma_start(win_t[:, :], w_in_t).then_inc(in_win, 16)
            sp.dma_start(xs[:, 1], x_rows[1]).then_inc(in_x[1], 16)
            sp.dma_start(bm_t[:, :, :], b_m_t).then_inc(in_bm, 16)
            sp.dma_start(win_x[:, :, :], w_in_x).then_inc(in_winx, 16)
            for b in range(2, B):
                sp.dma_start(xs[:, b], x_rows[b]).then_inc(in_x[b], 16)
            sp.dma_start(wout_t[:, :, :], w_out_t).then_inc(in_wout, 16)
            sp.dma_start(r1[:, :], router_w1).then_inc(in_r1, 16)
            sp.wait_ge(const_ready, 4)
            for j in range(STEPS):
                sp.dma_start(c_block[S * j:S * (j + 1), j, :], c_m).then_inc(in_c, 16)
            sp.dma_start(r2[:, 0, 0:E], router_w2).then_inc(in_r2, 16)
            sp.dma_start(r2[:, 1, E:2 * E], router_w2).then_inc(in_r2, 16)

            def load_expert_in(e):
                s = e % SLOTS
                if e >= SLOTS:
                    sp.wait_ge(ffn_mm, e - SLOTS + 1)
                sp.dma_start(experts[:, s, 0:DFF], w1[e]).then_inc(in_expert[s], 16)
                sp.dma_start(experts[:, s, DFF:2 * DFF], w2[e]).then_inc(in_expert[s], 16)

            def load_expert_out(e):
                s = e % SLOTS
                if e >= SLOTS and e % G == 0:
                    sp.wait_ge(eout_mm, (e - SLOTS) // G + 1)
                sp.dma_start(experts[:, s, 2 * DFF:].rearrange("p (f d) -> p f d", f=FH), w3[e]).then_inc(
                    in_expert_out[s], 16)

            for e in range(SLOTS):
                load_expert_in(e)
                load_expert_out(e)
            for n in range(UNITS):
                b, hf = n // 2, n % 2
                sp.wait_ge(xhat3_ready, n + 1)
                sp.dma_start(norm_by_chunk[b][:, hf * W:(hf + 1) * W],
                             xhat3[:, hf].rearrange("p j d -> p (j d)")).then_inc(stored[hf], 16)
            for g in range(SLOTS // G, NG):
                for e in range(G * g, G * (g + 1)):
                    load_expert_in(e)
                for e in range(G * g, G * (g + 1)):
                    load_expert_out(e)
            for n in range(UNITS):
                b, hf = n // 2, n % 2
                sp.wait_ge(final_ready, n + 1)
                sp.dma_start(out_rows[b][:, hf * W:(hf + 1) * W],
                             hs[:, b, hf * HALF:(hf + 1) * HALF, :].rearrange("p j d -> p (j d)")
                             ).then_inc(out_stored, 16)
            sp.wait_ge(out_stored, 16 * UNITS)

        @block.gpsimd
        def _(pool):
            order = Order(pool, pool_order)
            order.after(pool.memset(ident[:, :], 0.0))
            pool.affine_select(out=ident[:, :], in_=ident[:, :], compare_op=ALU.not_equal, fill=1.0, base=0,
                               pattern=[[-1, P]], channel_multiplier=1).then_inc(const_ready, 1)
            pool.memset(minus_half[:, :], -0.5).then_inc(const_ready, 1)

            def power(kind, b, j0, n, count=None):
                if count is not None:
                    pool.wait_ge(var_ready, count)
                r = rstd[:, kind, b, j0:j0 + n]
                ins = pool.tensor_tensor(r, var[:, kind, b, j0:j0 + n], minus_half[:, 0:n], ALU.pow)
                if kind != 1:
                    order.after(ins)
                    ins = pool.tensor_tensor(neg_shift[:, kind, b, j0:j0 + n], neg_mean[:, kind, b, j0:j0 + n], r,
                                             ALU.mult)
                ins.then_inc(rstd_ready, 1)

            pool.memset(r2[:, :, :], 0.0).then_inc(const_ready, 1)
            pool.memset(c_block[:, :, :], 0.0).then_inc(const_ready, 1)
            pool.wait_ge(const_ready, 2)
            power(0, 0, 0, STEPS, 1)
            pool.memset(into_pad[:, 0:PAD], 0.0).then_inc(const_ready, 1)
            pool.memset(last_pad[:, :, 0:PAD], 0.0).then_inc(const_ready, 1)
            order.after(pool.memset(select_last[:, :], 0.0))
            pool.affine_select(out=select_last[:, :], in_=select_last[:, :], compare_op=ALU.not_equal,
                               fill=1.0, base=PAD, pattern=[[-1, P]], channel_multiplier=1
                               ).then_inc(const_ready, 1)
            pool.memset(u[:, :, 0:HALO, 0:1], 0.0).then_inc(const_ready, 1)
            pool.memset(carry2[:, :, 0:1], 0.0).then_inc(const_ready, 1)
            pool.memset(carry1[:, :, 0:1], 0.0).then_inc(const_ready, 1)

            def per_row(table, b, n):
                return table[:, b, 0:D].unsqueeze(1).to_broadcast([P, n, D])

            def modulated(b):
                pool.wait_ge(mod_ready, b + 1)
                for hf in range(1 if b == 0 else 2):
                    pool.wait_ge(xhat_ready, 2 * b + hf + 1)
                    tiles = slice(hf * HALF, (hf + 1) * HALF)
                    order.after(pool.tensor_tensor(hs[:, b, tiles], xhat[:, tiles, :], per_row(scale_a, b, HALF),
                                                   ALU.mult))
                    pool.tensor_tensor(hs[:, b, tiles], hs[:, b, tiles], per_row(shift_a, b, HALF), ALU.add
                                       ).then_inc(h_ready, 1)

            def base(b):
                pool.wait_ge(xn_ready, 2 * (b + 1))
                pool.wait_ge(gates_ready, 1)
                order.after(pool.tensor_tensor(hs[:, b], hs[:, b], per_row(gates, b, STEPS), ALU.mult))
                pool.tensor_tensor(hs[:, b], hs[:, b], xs[:, b], ALU.add).then_inc(base_ready, 1)

            modulated(0)
            power(0, 1, 0, STEPS, VAR1[1])
            power(1, 0, 0, STEPS, VAR2[0])
            modulated(1)
            for b in range(2, B):
                power(0, b, 0, STEPS, VAR1[b])
            for b in range(1, B):
                power(1, b, 0, STEPS, VAR2[b])
                if b + 1 < B:
                    modulated(b + 1)
            for b in range(B):
                base(b)
            pool.wait_ge(xz_mm, 8 * B)
            pool.iota(token_of[:, :, :], pattern=[[1, STEPS], [STEPS, CH]], base=0, channel_multiplier=0,
                      allow_small_or_imprecise_dtypes=True).then_inc(const_ready, 1)
            pool.iota(batch_row[:, :, :], pattern=[[0, NG], [L, B]], base=0, channel_multiplier=0,
                      allow_small_or_imprecise_dtypes=True).then_inc(const_ready, 1)
            pool.iota(lane[:, :], pattern=[[0, 1]], base=0, channel_multiplier=1).then_inc(const_ready, 1)
            order.after(pool.memset(next_half[:, :], 0.0))
            pool.affine_select(out=next_half[:, :], in_=next_half[:, :], compare_op=ALU.not_equal,
                               fill=1.0, base=-E, pattern=[[-1, P]], channel_multiplier=1
                               ).then_inc(const_ready, 1)
            for n in range(UNITS):
                b, j0 = n // 2, (n % 2) * HALF
                pool.wait_ge(moments_ready, n + 1)
                pool.tensor_scalar(neg_mean[:, 2, b, j0:j0 + HALF], mean_var[:, j0:j0 + HALF, 0], -1.0, None, ALU.mult)
                order.after(pool.tensor_scalar(var[:, 2, b, j0:j0 + HALF], mean_var[:, j0:j0 + HALF, 1], LN_EPS, None,
                                               ALU.add))
                power(2, b, j0, HALF)

            pool.wait_ge(slots_ready, 1)
            pool.wait_ge(stored[0], 16 * B)
            pool.wait_ge(stored[1], 16 * B)
            for t in range(NG * B):
                pool.indirect_dma_start(
                    out=picked[:, t // B, t % B, :], out_offset=None, in_=norm_rows,
                    in_offset=bass.IndirectOffsetOnAxis(ap=slot_row[:, t:t + 1], axis=0),
                ).then_inc(picked_in[t // B], 16)
            for g in range(NG):
                pool.wait_ge(hi_ready, g + 1)
                pool.tensor_tensor(rest, value, parts[:, g, 0], ALU.subtract).then_inc(rest_ready, 1)
                pool.wait_ge(mid_ready, g + 1)
                pool.tensor_tensor(rest, rest, parts[:, g, 1], ALU.subtract).then_inc(rest_ready, 1)

        @block.scalar
        def _(act):
            def norm(kind, dst, src, b, j0, n, ready):
                act.wait_ge(rstd_ready, ready)
                for j in range(n):
                    ins = act.activation(dst(j), src(j), ACT.Identity, scale=rstd[:, kind, b, j0 + j:j0 + j + 1],
                                         bias=neg_shift[:, kind, b, j0 + j:j0 + j + 1])
                return ins

            def first_norm(b, hf):
                if b == 1 and hf == 1:
                    act.wait_ge(h0_ready, 1)
                elif b > 0:
                    act.wait_ge(h_ready, H_READY[b - 1][hf])
                norm(0, lambda j: xhat[:, hf * HALF + j, :], lambda j: xs[:, b, hf * HALF + j, :], b, hf * HALF,
                     HALF, VAR1[b]).then_inc(xhat_ready, 1)

            def transposed(b):
                for hf in range(2):
                    act.wait_ge(tr_done, 2 * b + hf + 1)
                    if b > 1:
                        act.wait_ge(xz_mm, 8 * (b - 1))
                    act.activation(xn_t[:, b % 2, hf * HALF:(hf + 1) * HALF, :], tr_bank[hf][:, :],
                                   ACT.Identity, scale=gamma, bias=beta).then_inc(xnt_ready, 1)

            def silu_conv(b, m):
                act.wait_ge(conv_done, 2 * b + m + 1)
                act.activation(conv[:, m, b], conv[:, m, b], ACT.Silu).then_inc(silu_done, 1)

            def power_step(r, k):
                n = 1 << k
                act.wait_ge(pow_mm, POW[r] + k + 1)
                ins = act.activation(powers[:, r, (n + 1) * S:(2 * n + 1) * S], small_bank[0:S, 0:n * S], ACT.Copy)
                if n == 4 and r < 2:
                    act.activation(powers[:, r + 1, S:2 * S], small_bank[0:S, 3 * S:4 * S], ACT.Copy)
                    ins = act.activation(plain[:, r + 1, 0, :], small_bank[0:S, 4 * S:5 * S], ACT.Copy)
                elif n < 4:
                    ins = act.activation(plain[:, r, k + 1, :], small_bank[0:S, n * S:(n + 1) * S], ACT.Copy)
                ins.then_inc(pow_ready, 1)

            act.wait_ge(in_vec, 16)
            act.activation(cond_s[:, :], cond, ACT.Silu).then_inc(cond_ready, 1)
            for b in range(B):
                if b == 1:
                    first_norm(0, 0)
                    first_norm(0, 1)
                act.wait_ge(mod_mm, b + 1)
                act.activation(scale_a[:, b, :], xz_bank[b][:, D:2 * D], ACT.Identity, bias=1.0)
                act.activation(shift_a[:, b, :], xz_bank[b][:, 0:D], ACT.Copy).then_inc(mod_ready, 1)
                act.activation(gates[:, b, :], xz_bank[b][:, 2 * D:4 * D], ACT.Copy).then_inc(raw_ready, 1)
            act.wait_ge(mod_mm, B + 1)
            act.activation(mod_b[:, 0, :], small_bank[:, 0:B], ACT.Copy)
            act.activation(mod_b[:, 1, :], small_bank[:, B:2 * B], ACT.Identity, bias=1.0
                           ).then_inc(mod_ready, 1)
            act.wait_ge(const_ready, 1)
            act.wait_ge(in_a, 16)
            for r in range(3):
                act.activation(powers[:, r, 0:S], ident[0:S, 0:S], ACT.Copy)
            act.activation(powers[:, 0, S:2 * S], apair[:, 1, :], ACT.Copy)
            act.activation(plain[:, 0, 0, :], apair[:, 0, :], ACT.Copy).then_inc(pow_ready, 1)
            for k in range(3):
                power_step(0, k)
            first_norm(1, 0)
            first_norm(1, 1)
            act.wait_ge(pow_mm, 4)
            act.activation(bin_w[:, :], small_bank[0:S, 0:D], ACT.Copy).then_inc(pow_ready, 1)
            act.wait_ge(pow_mm, 5)
            act.activation(into_pad[:, PAD:], small_bank[:, 0:P], ACT.Copy).then_inc(pow_ready, 1)

            transposed(0)
            for b in range(B):
                n = 8 * b
                for m in range(M):
                    for hf in range(2):
                        n += 1
                        act.wait_ge(xz_mm, n)
                        if b == 0:
                            act.wait_ge(const_ready, 8)
                        else:
                            act.wait_ge(conv_done, 2 * (b - 1) + m + 1)
                        src = xz_bank[(n - 1) % 4]
                        tiles = src[:, :].rearrange("p (j c) -> p j c", c=CH)
                        act.activation(u[:, m, HALO + hf * HALF:HALO + (hf + 1) * HALF, :], tiles, ACT.Copy)
                        if hf == 1:
                            act.activation(u[:, m, 0:HALO, 1:], tiles[:, HALF - HALO:, 0:CH - 1], ACT.Copy)
                        act.activation(conv[:, m, b, hf * W:(hf + 1) * W], src[:, :], ACT.Identity,
                                       scale=conv_w[:, CONV_TAPS * (m + 1) - 1:CONV_TAPS * (m + 1)],
                                       bias=conv_b[:, m:m + 1]).then_inc(xz_read, 1)
                        if b in (1, 2) and m + hf == 1:
                            power_step(b, m)
                    if b + 2 < B:
                        first_norm(b + 2, m)
                for k in range(2 * M):
                    hf, m = k // M, k % M
                    n += 1
                    act.wait_ge(xz_mm, n)
                    act.activation(gate_z[:, m, b, hf * W:(hf + 1) * W], xz_bank[(n - 1) % 4][:, :],
                                   ACT.Tanh, scale=0.5).then_inc(xz_read, 1)
                    if b in (1, 2) and k == 0:
                        power_step(b, 2)
                    if b == 2 and k == 2:
                        act.wait_ge(pow_mm, 12)
                        act.activation(last_pad[:, 0, PAD:], small_bank[:, 0:P], ACT.Copy)
                        act.activation(last_pad[:, 1, PAD:], small_bank[:, P:2 * P], ACT.Copy).then_inc(pow_ready, 1)
                    if b + 1 < B and k == 1:
                        transposed(b + 1)
                    if b == B - 1:
                        silu_conv(k // M, k % M)
            for b in range(2, B):
                for m in range(M):
                    silu_conv(b, m)

            def third_norm(k):
                b, hf = k // 2, k % 2
                if k >= 2:
                    act.wait_ge(tr3_done, k - 1)
                    act.wait_ge(stored[hf], 16 * (k // 2))
                norm(2, lambda j: xhat3[:, hf, j, :], lambda j: hs[:, b, hf * HALF + j, :], b, hf * HALF, HALF,
                     2 * B + k + 1).then_inc(xhat3_ready, 1)

            def second_modulation(k):
                b, hf = k // 2, k % 2
                act.wait_ge(tr3_done, k + 1)
                if k >= 2:
                    act.wait_ge(router_mm, k - 1)
                act.activation(h2_t[:, hf, :], tr3_bank[hf][:, :], ACT.Identity, scale=mod_b[:, 1, b:b + 1],
                               bias=mod_b[:, 0, b:b + 1]).then_inc(h2_ready, 1)

            def router_silu(k):
                b, hf = k // 2, k % 2
                act.wait_ge(router_mm, k + 1)
                act.wait_ge(base_ready, B)
                act.activation(routed[:, b, hf * HALF:(hf + 1) * HALF, :],
                               router_bank[hf][:, :].rearrange("p (j c) -> p j c", c=CH), ACT.Silu
                               ).then_inc(routed_ready, 1)

            for n in range(1, UNITS):
                if n >= 4:
                    router_silu(n - 4)
                if n >= 3:
                    second_modulation(n - 3)
                third_norm(n - 1)
            second_modulation(UNITS - 3)
            router_silu(UNITS - 4)
            second_modulation(UNITS - 2)
            third_norm(UNITS - 1)
            router_silu(UNITS - 3)
            second_modulation(UNITS - 1)
            router_silu(UNITS - 2)
            router_silu(UNITS - 1)
            act.wait_ge(max_ready, 1)
            act.wait_ge(index_ready, 1)
            act.activation(exps, logit_bank[:, :], ACT.Exp, bias=neg_max[:, 0:1],
                           accum_out=half_sum[:, 0:1]).then_inc(exp_ready, 1)
            act.wait_ge(max_ready, 2)
            act.activation(e_top[:, :], best[:, :], ACT.Exp, bias=neg_max[:, 1:2], accum_out=exp_top[:, 0:1])
            act.activation(half_part[:, :], half_max[:, :], ACT.Exp, bias=neg_max[:, 1:2]).then_inc(exp_ready, 1)

            def chosen_norm(g):
                act.wait_ge(ptr_done, g + 1)
                if g >= 2:
                    act.wait_ge(ffn_mm, G * (g - 1))
                for b in range(B):
                    ins = act.activation(picked_t[:, g % 2, :, b, :],
                                         ptr_bank[:, b * P:(b + 1) * P].rearrange("p (q c) -> p q c", q=G),
                                         ACT.Identity, scale=mod_b[:, 1, b:b + 1], bias=mod_b[:, 0, b:b + 1])
                ins.then_inc(pickt_ready, 1)

            def part(g, i):
                if i == 0:
                    act.wait_ge(value_ready, g + 1)
                    act.activation(parts[:, g, 0], value, ACT.Copy).then_inc(hi_ready, 1)
                elif i == 1:
                    act.wait_ge(rest_ready, 2 * g + 1)
                    act.activation(parts[:, g, 1], rest, ACT.Copy).then_inc(mid_ready, 1)
                else:
                    act.wait_ge(rest_ready, 2 * g + 2)
                    act.activation(parts[:, g, 2], rest, ACT.Copy).then_inc(lo_ready, 1)

            chosen_norm(0)
            for e in range(E):
                g, q = e // G, e % G
                act.wait_ge(ffn_mm, e + 1)
                if e >= FFN_BUFS:
                    act.wait_ge(hidden_ready, e - FFN_BUFS + 1)
                act.activation(silu_g[:, e % FFN_BUFS, :], ffn_bank[e % FFN_BUFS][:, 0:FH * P], ACT.Silu
                               ).then_inc(silu_g_ready, 1)
                if g >= 1 and q == G - 1:
                    part(g - 1, 0)
                if g >= 2 and q < 2:
                    part(g - 2, q + 1)
                if q == 1 and g + 1 < NG:
                    chosen_norm(g + 1)
            part(NG - 2, 1)
            part(NG - 2, 2)
            for i in range(3):
                part(NG - 1, i)

        @block.tensor
        def _(pe):
            pe.wait_ge(in_wmod, 16)
            for b in range(B):
                pe.wait_ge(cond_rows_ready, b + 1)
                pe.matmul(xz_bank[b][:, 0:3 * D], cond_rows[:, b, :], wmod[:, 0:3 * D], start=True, stop=True)
                pe.matmul(xz_bank[b][:, 3 * D:4 * D], cond_rows[:, b, :], wmod[:, 5 * D:6 * D], start=True,
                          stop=True).then_inc(mod_mm, 1)
            pe.matmul(small_bank[:, 0:B], wmod[:, 3 * D:4 * D], cond_s[:, :], start=True, stop=True)
            pe.matmul(small_bank[:, B:2 * B], wmod[:, 4 * D:5 * D], cond_s[:, :], start=True, stop=True
                      ).then_inc(mod_mm, 1)

            def power_product(r, k):
                tb, n = powers[:, r, :], 1 << k
                pe.wait_ge(pow_ready, POW[r] + k + 1)
                pe.matmul(small_bank[0:S, 0:n * S], plain[:, r, k, :], tb[:, S:(n + 1) * S], start=True, stop=True)
                pe.matmul(small_bank[0:S, n * S:(n + 1) * S], tb[:, n * S:(n + 1) * S], plain[:, r, k, :],
                          start=True, stop=True).then_inc(pow_mm, 1)

            for k in range(3):
                power_product(0, k)
            pe.wait_ge(in_bm, 16)
            pe.wait_ge(in_winx, 16)
            pe.wait_ge(pow_ready, 4)
            for m in range(M):
                ins = pe.matmul(small_bank[0:S, 0:D], bm_t[:, m, :], win_x[:, m, :], start=(m == 0),
                                stop=(m == M - 1))
            ins.then_inc(pow_mm, 1)
            pe.wait_ge(pow_ready, 5)
            pe.matmul(small_bank[:, 0:P], bin_w[:, :], powers[:, 0, 0:P], start=True, stop=True).then_inc(pow_mm, 1)

            y1v = y1[:, :, :].rearrange("p b (C i) -> p b C i", i=STEPS)
            y2v = y2[:, :, :].rearrange("p b (g i) -> p b g i", i=STEPS)
            c2 = small_bank[0:S, 128:128 + 16 * B].rearrange("p (b C) -> p b C", b=B)
            c1 = tr_bank[0][0:S, :].rearrange("p (b C) -> p b C", b=B)

            def scan_product(k):
                pe.wait_ge(scan_step, k + 1)
                if k == 0:
                    pe.wait_ge(pow_ready, 13)
                    pe.wait_ge(const_ready, 6)
                    for i in range(STEPS):
                        ins = pe.matmul(small_bank[:, 0:B * 16], last_pad[:, 0, PAD - S * i:PAD - S * i + P],
                                        y1v[:, :, :, i], start=(i == 0), stop=(i == STEPS - 1))
                elif k == 1:
                    for i in range(STEPS):
                        ins = pe.matmul(small_bank[:, 64:64 + 2 * B], last_pad[:, 1, PAD - S * i:PAD - S * i + P],
                                        y2v[:, :, :, i], start=(i == 0), stop=(i == STEPS - 1))
                elif k == 2:
                    ins = pe.matmul(small_bank[0:S, 72:72 + B], ident[:, PAD:P], y3[:, :, 0], start=True, stop=True)
                elif k == 3:
                    ins = pe.matmul(small_bank[:, 76:76 + B], powers[:, 2, S:], carry3[:, :], start=True, stop=True)
                elif k == 4:
                    for i in range(STEPS):
                        n = 2 if i < STEPS - 1 else 1
                        ins = pe.matmul(c2[:, :, i + 1:i + 1 + STEPS * (n - 1) + 1:STEPS],
                                        ident[:, S * i:S * (i + 1)], y3[:, :, 0:n], start=True, stop=True)
                elif k == 5:
                    ins = pe.matmul(small_bank[:, 192:192 + 16 * B], powers[:, 1, S:],
                                    carry2[:, :, :].rearrange("p b C -> p (b C)"), start=True, stop=True)
                elif k == 6:
                    for i in range(STEPS):
                        n = 16 if i < STEPS - 1 else 15
                        ins = pe.matmul(c1[:, :, i + 1:i + 1 + STEPS * (n - 1) + 1:STEPS],
                                        ident[:, S * i:S * (i + 1)], y2[:, :, 0:n], start=True, stop=True)
                else:
                    ins = pe.matmul(tr_bank[1][:, :], powers[:, 0, S:], carry1[:, :, :].rearrange("p b C -> p (b C)"),
                                    start=True, stop=True)
                ins.then_inc(scan_mm, 1)

            pe.wait_ge(in_win, 16)
            for b in range(B):
                for hf in range(2):
                    pe.wait_ge(xn_ready, 2 * b + hf + 1)
                    if b > 0:
                        pe.wait_ge(xnt_ready, 2 * (b - 1) + hf + 1)
                    for k in range(HALF):
                        ins = pe.transpose(tr_bank[hf][:, k * P:(k + 1) * P], xn[:, hf * HALF + k, :],
                                           ident[:, :])
                    ins.then_inc(tr_done, 1)
                n = 8 * b

                def take_bank(n):
                    if n >= 4:
                        pe.wait_ge(xz_read, n - 3)
                    elif n == 0:
                        pe.wait_ge(raw_ready, B)
                    return xz_bank[n % 4]

                def x_part(m, hf):
                    pe.wait_ge(xnt_ready, 2 * b + hf + 1)
                    pe.matmul(take_bank(n)[:, :], win_t[:, m * P:(m + 1) * P],
                              xn_t[:, b % 2, hf * HALF:(hf + 1) * HALF, :], start=True, stop=True
                              ).then_inc(xz_mm, 1)

                x_part(0, 0)
                n += 1
                x_part(0, 1)
                n += 1
                if b in (1, 2):
                    power_product(b, 0)
                if b == 0:
                    pe.wait_ge(pow_ready, 6)
                    pe.wait_ge(const_ready, 5)
                for i in range(STEPS):
                    ins = pe.matmul(y_bank[:, b * CH:(b + 1) * CH], into_pad[:, PAD - S * i:PAD - S * i + P],
                                    xn_t[:, b % 2, i, :], start=(i == 0), stop=(i == STEPS - 1))
                ins.then_inc(scan_in, 1)
                for hf in range(2):
                    x_part(1, hf)
                    n += 1
                    if b in (1, 2) and hf == 0:
                        power_product(b, 1)
                    if b == B - 1:
                        scan_product(hf)
                for k in range(2 * M):
                    hf, m = k // M, k % M
                    pe.matmul(take_bank(n)[:, :], win_t[:, INNER + m * P:INNER + (m + 1) * P],
                              xn_t[:, b % 2, hf * HALF:(hf + 1) * HALF, :], start=True, stop=True
                              ).then_inc(xz_mm, 1)
                    n += 1
                    if b in (1, 2) and k == 0:
                        power_product(b, 2)
                    if b == 2 and k == 2:
                        pe.wait_ge(pow_ready, 12)
                        pe.wait_ge(const_ready, 7)
                        for r in (1, 2):
                            ins = pe.matmul(small_bank[:, (r - 1) * P:r * P], select_last[:, :],
                                            powers[:, r, 0:P], start=True, stop=True)
                        ins.then_inc(pow_mm, 1)
                    if b == B - 1:
                        scan_product(2 + k)
            scan_product(6)
            scan_product(7)

            pe.wait_ge(in_c, 16 * STEPS)
            pe.wait_ge(xz_read, 8 * B - 2)
            def logits_of(batches):
                for h in range(2):
                    for b in batches:
                        ins = pe.matmul(logit_bank[32 * b:32 * b + 32, :], r2[:, h, :],
                                        routed[:, b, :, h * (CH // 2):(h + 1) * (CH // 2)].rearrange("p j c -> p c j"),
                                        start=(h == 0), stop=(h == 1))
                return ins

            def normalised(k):
                pe.wait_ge(xhat3_ready, k + 1)
                if k >= 2:
                    pe.wait_ge(h2_ready, k - 1)
                for j in range(HALF):
                    ins = pe.transpose(tr3_bank[k % 2][:, j * P:(j + 1) * P], xhat3[:, k % 2, j, :], ident[:, :])
                ins.then_inc(tr3_done, 1)

            def router(k):
                pe.wait_ge(h2_ready, k + 1)
                pe.wait_ge(in_r1, 16)
                if k >= 2:
                    pe.wait_ge(routed_ready, k - 1)
                pe.matmul(router_bank[k % 2][:, :], r1[:, :], h2_t[:, k % 2, :], start=True, stop=True
                          ).then_inc(router_mm, 1)

            for n in range(UNITS + 1):
                if n < UNITS:
                    b, hf = n // 2, n % 2
                    if n == 0:
                        pe.wait_ge(state_ready, 1)
                    for m in range(M):
                        if n > 0:
                            pe.wait_ge(sc_read, 2 * n + m - 1)
                        for k in range(HALF):
                            ins = pe.matmul(sc_bank[m][:, k * CH:(k + 1) * CH],
                                            c_block[:, hf * HALF + k, m * P:(m + 1) * P], y1[:, b, :],
                                            start=True, stop=True)
                        ins.then_inc(sc_mm, 1)
                if n >= 1:
                    k1 = n - 1
                    b = k1 // 2
                    pe.wait_ge(y_ready, 2 * (k1 + 1))
                    pe.wait_ge(wout_ready, B)
                    if k1 >= 1:
                        pe.wait_ge(x1_ready, k1)
                    else:
                        pe.wait_ge(xz_read, 8 * B)
                    for k in range(HALF):
                        for m in range(M):
                            ins = pe.matmul(out_bank[:, k * D:(k + 1) * D], y[:, k1 % 2, m, k * P:(k + 1) * P],
                                            wout_g[:, b, m, :], start=(m == 0), stop=(m == M - 1))
                    ins.then_inc(out_mm, 1)
                if n >= 4:
                    router(n - 4)
                if n >= 3:
                    normalised(n - 3)
            pe.wait_ge(in_r2, 32)
            pe.wait_ge(routed_ready, UNITS // 2)
            logits_of(range(B // 2))
            normalised(UNITS - 2)
            router(UNITS - 3)
            router(UNITS - 2)
            normalised(UNITS - 1)
            router(UNITS - 1)
            pe.wait_ge(routed_ready, UNITS)
            logits_of(range(B // 2, B)).then_inc(logits_mm, 1)
            pe.wait_ge(const_ready, 14)
            pe.wait_ge(found_ready, 1)
            pe.matmul(other_bank[:, 0:2 * CAPACITY], next_half[:, :], found[:, :], start=True, stop=True
                      ).then_inc(other_mm, 1)
            pick = ident[:, :].rearrange("p (b r q) -> p q r b", b=B, q=G)
            for what, src in enumerate((best_token, w_top)):
                pe.wait_ge(weights_ready, what + 1)
                for q in range(G):
                    ins = pe.matmul(slot_bank[what][32 * q:32 * q + 32, 0:NG * B], src[:, :],
                                    pick[:, q, 0:NG, :], start=True, stop=True)
                ins.then_inc(slots_mm, 1)
                if what == 0:
                    pe.wait_ge(exp_ready, 1)
                    pe.wait_ge(merged, 1)
                    pe.matmul(other_bank[:, 2 * CAPACITY:2 * CAPACITY + 1], next_half[:, :], half_sum[:, 0:1],
                              start=True, stop=True).then_inc(other_mm, 1)

            def pick_transposes(g):
                pe.wait_ge(picked_in[g], 16 * B)
                if g >= 1:
                    pe.wait_ge(pickt_ready, g)
                for b in range(B):
                    ins = pe.transpose(ptr_bank[:, b * P:(b + 1) * P], picked[:, g, b, :], ident[:, :])
                ins.then_inc(ptr_done, 1)

            def expert_out(g):
                pe.wait_ge(hidden_ready, G * (g + 1))
                for q in range(G):
                    s = (g * G + q) % SLOTS
                    pe.wait_ge(in_expert_out[s], 16 * ((g * G + q) // SLOTS + 1))
                if g >= 1:
                    pe.wait_ge(value_ready, g)
                for b in range(B):
                    for f in range(FH):
                        for q in range(G):
                            s = (g * G + q) % SLOTS
                            w3_s = experts[:, s, 2 * DFF + f * D:2 * DFF + (f + 1) * D]
                            ins = pe.matmul(eout_bank[32 * q:32 * q + 32, b * D:(b + 1) * D],
                                            hidden[:, q, f, b * CAPACITY:(b + 1) * CAPACITY], w3_s,
                                            start=(f == 0), stop=(f == FH - 1))
                ins.then_inc(eout_mm, 1)

            def scatter(n, g):
                b, hf = n // 2, n % 2
                pe.wait_ge(onehot_ready, B * (g + 1))
                pe.wait_ge(lo_ready, g + 1)
                for k in range(HALF):
                    j = hf * HALF + k
                    for i in range(3):
                        ins = pe.matmul(scatter_bank[n][:, k * D:(k + 1) * D],
                                        onehot[:, g, b, j * CH:(j + 1) * CH], parts[:, g, i, b, :],
                                        start=(g == 0 and k == 0 and i == 0),
                                        stop=(g == NG - 1 and k == HALF - 1 and i == 2))
                return ins

            EARLY, AHEAD = 3, 6
            pick_transposes(0)
            for e in range(E):
                g, q, s = e // G, e % G, e % SLOTS
                pe.wait_ge(in_expert[s], 32 * (e // SLOTS + 1))
                pe.wait_ge(pickt_ready, g + 1)
                if e == 0:
                    pe.wait_ge(slots_ready, 2)
                if e >= FFN_BUFS:
                    pe.wait_ge(hidden_ready, e - FFN_BUFS + 1)
                for half in range(2):
                    for f in range(FH):
                        at = half * DFF + f * P
                        ins = pe.matmul(ffn_bank[e % FFN_BUFS][:, (half * FH + f) * P:(half * FH + f + 1) * P],
                                        experts[:, s, at:at + P], picked_t[:, g % 2, q], start=True,
                                        stop=True)
                ins.then_inc(ffn_mm, 1)
                if q == 1:
                    if g + 1 < NG:
                        pick_transposes(g + 1)
                    if g >= 1:
                        expert_out(g - 1)
                if q == G - 1 and g >= 2:
                    for n in range(EARLY):
                        scatter(n, g - 2)
            expert_out(NG - 1)

            pe.wait_ge(hidden_ready, E)
            for n in range(EARLY, AHEAD):
                for g in range(NG - 2):
                    scatter(n, g)
            for n in range(AHEAD):
                scatter(n, NG - 2)
            for n in range(AHEAD):
                scatter(n, NG - 1).then_inc(scatter_mm, 1)
            pe.wait_ge(value_ready, NG)
            for n in range(AHEAD, UNITS):
                for g in range(NG):
                    ins = scatter(n, g)
                ins.then_inc(scatter_mm, 1)

        @block.vector
        def _(dve):
            order = Order(dve, dve_order)
            dve.memset(ones[:, :], 1.0).then_inc(ones_ready, 1)

            def ln_stats(kind, src, stats, b, j0, n):
                for j in range(n):
                    if kind == 0 and b == 0 and j % HALF == 0:
                        dve.wait_ge(in_x[0] if j == 0 else in_x0_rest, 16)
                    if kind == 1 and j % HALF == 0:
                        if b == 0 and j == HALF:
                            dve.wait_ge(h0_ready, 1)
                        else:
                            dve.wait_ge(h_ready, H_READY[b][j // HALF])
                    ins = dve.bn_stats(stats[:, j, :], src(j))
                order.after(ins)
                for j in range(n):
                    ins = dve.bn_aggr(mean_var[:, j, :], stats[:, j, :])
                order.after(ins)
                dve.tensor_scalar(neg_mean[:, kind, b, j0:j0 + n], mean_var[:, 0:n, 0], -1.0, None, ALU.mult)
                dve.tensor_scalar(var[:, kind, b, j0:j0 + n], mean_var[:, 0:n, 1], LN_EPS, None, ALU.add
                                  ).then_inc(var_ready, 1)

            def second_norm(b):
                dve.wait_ge(rstd_ready, VAR2[b])
                if b > 0:
                    dve.wait_ge(tr_done, 2 * b)
                for j in range(STEPS):
                    ins = dve.tensor_scalar(xn[:, j, :], hs[:, b, j, :], neg_mean[:, 1, b, j:j + 1],
                                            rstd[:, 1, b, j:j + 1], ALU.add, ALU.mult)
                    if j % HALF == HALF - 1:
                        ins.then_inc(xn_ready, 1)

            def stats_a(b):
                if b > 0:
                    dve.wait_ge(in_x[b], 16)
                ln_stats(0, lambda j: xs[:, b, j, :], st1, b, 0, STEPS)

            def conv_tap(b, m, s):
                if s == 1:
                    dve.wait_ge(xz_read, 8 * b + 2 * m + 2)
                else:
                    dve.wait_ge(tap_done, 2 * (2 * b + m) + s - 1)
                acc = conv[:, m, b].rearrange("p (j c) -> p j c", c=CH)
                dve.scalar_tensor_tensor(out=acc, in0=u[:, m, HALO - s:HALO - s + STEPS, :],
                                         scalar=conv_w[:, CONV_TAPS * (m + 1) - 1 - s:CONV_TAPS * (m + 1) - s],
                                         in1=acc, op0=ALU.mult, op1=ALU.add
                                         ).then_inc(tap_done if s < CONV_TAPS - 1 else conv_done, 1)

            def conv_taps(b, m):
                for s in range(1, CONV_TAPS):
                    conv_tap(b, m, s)

            dve.wait_ge(ones_ready, 1)
            dve.wait_ge(cond_ready, 1)
            for b in range(B):
                dve.tensor_scalar(cond_rows[:, b, :], ones[:, :], cond_s[:, b:b + 1], None, ALU.mult
                                  ).then_inc(cond_rows_ready, 1)
            stats_a(0)
            stats_a(1)
            second = slice(HALF, STEPS)
            dve.wait_ge(mod_ready, 1)
            dve.wait_ge(xhat_ready, 2)
            order.after(dve.tensor_tensor(hs[:, 0, second], xhat[:, second, :],
                                          scale_a[:, 0, :].unsqueeze(1).to_broadcast([P, HALF, D]), ALU.mult))
            dve.tensor_tensor(hs[:, 0, second], hs[:, 0, second],
                              shift_a[:, 0, :].unsqueeze(1).to_broadcast([P, HALF, D]), ALU.add
                              ).then_inc(h0_ready, 1)
            for b in range(B):
                ln_stats(1, lambda j: hs[:, b, j, :], st2, b, 0, STEPS)
                if b == 0:
                    stats_a(2)
                else:
                    conv_taps(b - 1, 0)
                second_norm(b)
                if b > 0:
                    conv_taps(b - 1, 1)
                if b == 0:
                    stats_a(3)
            def hold_gate(which, place):
                raw = gates[:, :, which * D:(which + 1) * D]
                sign, size = place[:, 0], place[:, 1]
                if which == 0:
                    dve.wait_ge(raw_ready, B)
                order.after(dve.tensor_scalar(sign, raw, 0.0, 2.0, ALU.is_ge, ALU.mult))
                order.after(dve.scalar_tensor_tensor(out=size, in0=sign, scalar=-1.0, in1=raw, op0=ALU.add,
                                                     op1=ALU.mult))
                order.after(dve.tensor_scalar(size, size, 0.25, None, ALU.max))
                dve.scalar_tensor_tensor(out=raw, in0=sign, scalar=-1.0, in1=size, op0=ALU.add,
                                         op1=ALU.mult).then_inc(gates_ready, 1)

            def gated_w_out(b):
                if b == 0:
                    dve.wait_ge(in_wout, 16)
                    dve.wait_ge(gates_ready, 1)
                for m in range(M):
                    ins = dve.scalar_tensor_tensor(out=wout_g[:, b, m, :], in0=wout_t[:, m, :], scalar=0.5,
                                                   in1=gates[:, b, 0:D], op0=ALU.mult, op1=ALU.mult)
                ins.then_inc(wout_ready, 1)

            def columns(t):
                return t[:, :, :].rearrange("p b C -> p (b C)")

            dve.wait_ge(scan_in, B)
            dve.tensor_copy(columns(y1), y_bank[:, :]).then_inc(scan_step, 1)
            hold_gate(0, gate_a_parts)
            dve.wait_ge(scan_mm, 1)
            dve.tensor_copy(columns(y2), small_bank[:, 0:16 * B]).then_inc(scan_step, 1)
            conv_tap(B - 1, 0, 1)
            dve.wait_ge(scan_mm, 2)
            dve.tensor_copy(columns(y3), small_bank[:, 64:64 + 2 * B]).then_inc(scan_step, 1)
            gated_w_out(0)
            gated_w_out(1)
            dve.wait_ge(scan_mm, 3)
            dve.tensor_copy(carry3[:, :], small_bank[0:S, 72:72 + B]).then_inc(scan_step, 1)
            gated_w_out(2)
            dve.wait_ge(scan_mm, 4)
            dve.tensor_tensor(y3[:, :, 1], y3[:, :, 1], small_bank[:, 76:76 + B], ALU.add).then_inc(scan_step, 1)
            gated_w_out(3)
            dve.wait_ge(scan_mm, 5)
            dve.wait_ge(const_ready, 10)
            dve.tensor_copy(carry2[:, :, 1:], small_bank[0:S, 128:128 + 16 * B].rearrange(
                "p (b C) -> p b C", b=B)[:, :, 1:]).then_inc(scan_step, 1)
            conv_tap(B - 1, 0, 2)
            dve.wait_ge(scan_mm, 6)
            dve.tensor_tensor(columns(y2), columns(y2), small_bank[:, 192:192 + 16 * B], ALU.add).then_inc(scan_step, 1)
            dve.wait_ge(scan_mm, 7)
            dve.tensor_copy(carry1[:, :, 1:], tr_bank[0][0:S, :].rearrange("p (b C) -> p b C", b=B)[:, :, 1:]
                            ).then_inc(scan_step, 1)
            conv_tap(B - 1, 0, 3)
            dve.wait_ge(scan_mm, 8)
            dve.tensor_tensor(columns(y1), columns(y1), tr_bank[1][:, :], ALU.add).then_inc(state_ready, 1)
            conv_tap(B - 1, 1, 1)
            conv_tap(B - 1, 1, 2)

            for n in range(UNITS + 1):
                if n < UNITS:
                    b, hf = n // 2, n % 2
                    cols = slice(hf * W, (hf + 1) * W)
                    dve.wait_ge(silu_done, 2 * (b + 1))
                    dve.wait_ge(xz_read, 8 * (b + 1))
                    for m in range(M):
                        dve.wait_ge(sc_mm, 2 * n + m + 1)
                        dve.tensor_tensor(conv[:, m, b, cols], conv[:, m, b, cols], sc_bank[m][:, :],
                                          ALU.add).then_inc(sc_read, 1)
                    if n >= 2:
                        dve.wait_ge(out_mm, n - 1)
                    for m in range(M):
                        dve.wait_ge(sc_read, 2 * n + m + 1)
                        dve.scalar_tensor_tensor(out=y[:, n % 2, m, :], in0=gate_z[:, m, b, cols], scalar=1.0,
                                                 in1=conv[:, m, b, cols], op0=ALU.add, op1=ALU.mult
                                                 ).then_inc(y_ready, 1)
                    if n == 0:
                        conv_tap(B - 1, 1, 3)
                if 1 <= n <= UNITS:
                    k1 = n - 1
                    b, hf = k1 // 2, k1 % 2
                    dve.wait_ge(out_mm, k1 + 1)
                    dve.wait_ge(base_ready, b + 1)
                    rows = hs[:, b, hf * HALF:(hf + 1) * HALF, :].rearrange("p j d -> p (j d)")
                    dve.tensor_tensor(rows, rows, out_bank[:, :], ALU.add).then_inc(x1_ready, 1)
                    dve.wait_ge(x1_ready, k1 + 1)
                    if k1 >= 2:
                        dve.wait_ge(rstd_ready, 2 * B + k1 - 1)
                    for j in range(HALF):
                        ins = dve.bn_stats(st1[:, hf * HALF + j, :], hs[:, b, hf * HALF + j, :])
                    order.after(ins)
                    for j in range(HALF):
                        ins = dve.bn_aggr(mean_var[:, hf * HALF + j, :], st1[:, hf * HALF + j, :])
                    ins.then_inc(moments_ready, 1)

            dve.wait_ge(out_mm, UNITS)
            hold_gate(1, gate_b_parts)
            dve.wait_ge(const_ready, 13)
            order.after(dve.tensor_scalar(lane[:, :], lane[:, :], E, None, ALU.bitwise_and))
            order.after(dve.tensor_scalar(half_start[:, :], lane[:, :], float(L // 2 // E), None, ALU.mult))
            dve.wait_ge(logits_mm, 1)
            rounds = CAPACITY // 8
            for r in range(rounds):
                src = logit_bank[:, :] if r == 0 else left[(r - 1) % 2]
                eight = found[:, 8 * r:8 * r + 8]
                if r > 0:
                    dve.wait_ge(left_ready, r)
                order.after(dve.max(eight, src))
                if r == 0:
                    dve.tensor_scalar(neg_max[:, 0:1], found[:, 0:1], -1.0, None, ALU.mult).then_inc(max_ready, 1)
                if r + 1 < rounds:
                    dve.match_replace(left[r % 2], eight, src, LOWEST).then_inc(left_ready, 1)
                dve.max_index(found_at[:, 8 * r:8 * r + 8], eight, src).then_inc(index_ready, 1)
            dve.wait_ge(index_ready, rounds)
            dve.tensor_scalar(found[:, CAPACITY:], found_at[:, :], half_start[:, 0:1], None, ALU.add
                              ).then_inc(found_ready, 1)
            dve.wait_ge(other_mm, 1)
            other = other_bank[:, CAPACITY - 1::-1]
            other_token = other_bank[:, 2 * CAPACITY - 1:CAPACITY - 1:-1]
            dve.tensor_tensor(keep[:, :], found[:, 0:CAPACITY], other, ALU.is_ge)
            dve.tensor_tensor(best[:, :], found[:, 0:CAPACITY], other, ALU.max)
            order.after(dve.tensor_tensor(best_token[:, :], found[:, CAPACITY:], other_token, ALU.subtract))
            order.after(dve.tensor_tensor(best_token[:, :], best_token[:, :], keep[:, :], ALU.mult))
            dve.tensor_tensor(best_token[:, :], best_token[:, :], other_token, ALU.add).then_inc(weights_ready, 1)
            dve.tensor_copy(half_max[:, 0:1], found[:, 0:1])
            order.after(dve.tensor_copy(half_max[:, 1:2], other_bank[:, 0:1]))
            merged_at = dve.tensor_tensor(neg_max[:, 1:2], half_max[:, 0:1], half_max[:, 1:2], ALU.max)
            merged_at.then_inc(merged, 1)
            dve.wait_ge(slots_mm, 1)
            dve.wait_ge(const_ready, 12)
            dve.tensor_tensor(slot_row[:, :], slot_bank[0][:, 0:NG * B], batch_row[:, :, :].rearrange("p g b -> p (g b)"),
                              ALU.add).then_inc(slots_ready, 1)
            dve.tensor_copy(slot_at[:, 0, :], slot_bank[0][:, 0:NG * B])
            dve.wait_ge(merged, 1)
            dve.tensor_scalar(neg_max[:, 1:2], neg_max[:, 1:2], -1.0, None, ALU.mult).then_inc(max_ready, 1)
            dve.wait_ge(other_mm, 2)
            order.after(dve.tensor_copy(half_sum[:, 1:2], other_bank[:, 2 * CAPACITY:2 * CAPACITY + 1]))
            dve.wait_ge(exp_ready, 2)
            order.after(dve.tensor_tensor(exp_all[:, :], half_part[:, :], half_sum[:, :], ALU.mult))
            order.after(dve.tensor_tensor(exp_all[:, 0:1], exp_all[:, 0:1], exp_all[:, 1:2], ALU.add))
            order.after(dve.reciprocal(rz[:, :], exp_all[:, 0:1]))
            order.after(dve.tensor_scalar(den[:, :], exp_top[:, :], rz[:, 0:1], 1e-9, ALU.mult, ALU.add))
            order.after(dve.reciprocal(rden[:, :], den[:, :]))
            dve.tensor_scalar(w_top[:, :], e_top[:, :], rz[:, 0:1], rden[:, 0:1], ALU.mult, ALU.mult
                              ).then_inc(weights_ready, 1)
            dve.wait_ge(slots_mm, 2)
            dve.tensor_copy(slot_at[:, 1, :], slot_bank[1][:, 0:NG * B]).then_inc(slots_ready, 1)
            dve.wait_ge(slots_ready, 2)

            def one_hot(t):
                dve.tensor_scalar(onehot[:, t // B, t % B, :], token_of[:, :, :].rearrange("p j c -> p (j c)"),
                                  slot_at[:, 0, t:t + 1], None, ALU.is_equal).then_inc(onehot_ready, 1)

            def expert_value(g):
                dve.wait_ge(eout_mm, g + 1)
                if g >= 1:
                    dve.wait_ge(lo_ready, g)
                else:
                    dve.wait_ge(gates_ready, 2)
                for b in range(B):
                    ins = dve.scalar_tensor_tensor(out=value[:, b, :], in0=eout_bank[:, b * D:(b + 1) * D],
                                                   scalar=slot_at[:, 1, g * B + b:g * B + b + 1],
                                                   in1=gates[:, b, D:2 * D], op0=ALU.mult, op1=ALU.mult)
                ins.then_inc(value_ready, 1)

            for t in range((NG - 1) * B):
                one_hot(t)
            for e in range(E):
                g, q = e // G, e % G
                if g == 0:
                    one_hot((NG - 1) * B + q)
                dve.wait_ge(silu_g_ready, e + 1)
                if e >= G and q == 0:
                    dve.wait_ge(eout_mm, g)
                dve.tensor_tensor(hidden[:, q].rearrange("p f t -> p (f t)"), silu_g[:, e % FFN_BUFS, :],
                                  ffn_bank[e % FFN_BUFS][:, FH * P:2 * FH * P], ALU.mult).then_inc(hidden_ready, 1)
                if g >= 1 and q == 2:
                    expert_value(g - 1)
            expert_value(NG - 1)
            for n in range(UNITS):
                b, hf = n // 2, n % 2
                dve.wait_ge(scatter_mm, n + 1)
                rows = hs[:, b, hf * HALF:(hf + 1) * HALF, :].rearrange("p j d -> p (j d)")
                dve.tensor_tensor(rows, rows, scatter_bank[n][:, :], ALU.add).then_inc(final_ready, 1)


def kernel(**inputs):
    import numpy as np
    import concourse.bacc as bacc
    from concourse.bass_utils import run_bass_kernel_spmd

    a = {n: np.ascontiguousarray(v) for n, v in inputs.items()}
    t = np.ascontiguousarray
    d = a["L0_attn_x"].shape[-1]
    inner = a["L0_attn_conv_w"].shape[0]
    m = inner // d
    vectors = np.concatenate([
        a["L0_c"].T, a["L0_attn_ln_gamma"][:, None], a["L0_attn_ln_beta"][:, None],
        a["L0_attn_conv_b"].reshape(m, d).T,
        a["L0_attn_conv_w"].reshape(m, d, -1).transpose(1, 0, 2).reshape(d, -1)], axis=1)
    arrays = dict(
        x=a["L0_attn_x"], vectors=t(vectors), w_mod=a["L0_wmod"],
        w_in_t=t(a["L0_attn_W_in"].T),
        w_in_x=t(a["L0_attn_W_in"][:inner].reshape(m, d, d).transpose(1, 0, 2)),
        w_out_t=t(a["L0_attn_W_out"].T.reshape(m, d, d).transpose(1, 0, 2)),
        a_pair=t(np.stack([a["L0_attn_A"], a["L0_attn_A"].T], axis=1)),
        c_m=a["L0_attn_Cm"],
        b_m_t=t(a["L0_attn_Bm"].T.reshape(m, d, -1).transpose(1, 0, 2)),
        router_w1=a["L0_ffn_router_w1"], router_w2=a["L0_ffn_router_w2"],
        w1=a["L0_ffn_w1"], w2=a["L0_ffn_w2"],
        w3=t(a["L0_ffn_w3"].reshape(a["L0_ffn_w3"].shape[0], -1, d, d).transpose(0, 2, 1, 3)),
    )
    nc = bacc.Bacc("TRN2", target_bir_lowering=False, num_devices=1)
    args = {n: nc.dram_tensor(f"in_{n}", v.shape, mybir.dt.from_np(v.dtype), kind="ExternalInput").ap()
            for n, v in arrays.items()}
    out = nc.dram_tensor("out_0", arrays["x"].shape, F32, kind="ExternalOutput").ap()
    adaln_block(nc, out=out, **args)
    r = run_bass_kernel_spmd(nc, [{f"in_{n}": v for n, v in arrays.items()}], core_ids=[0])
    return r.results[0]["out_0"]
```

```python
from contextlib import ExitStack

import concourse.bass as bass
from concourse import mybir

F32 = mybir.dt.float32
BF16 = mybir.dt.bfloat16
U32 = mybir.dt.uint32
I32 = mybir.dt.int32
ALU = mybir.AluOpType
ACT = mybir.ActivationFunctionType

P = 128
STEPS = 8
LN_EPS = 1e-5
CAPACITY = 32
CONV_TAPS = 4
LOWEST = -3.4028234e38


class Order:

    def __init__(self, eng, sem):
        self.eng, self.sem, self.at = eng, sem, 0

    def after(self, ins):
        self.at += 1
        ins.then_inc(self.sem, 1)
        self.eng.wait_ge(self.sem, self.at)


def adaln_block(nc, x, vectors, w_mod, w_in_t, w_in_x, w_out_t, a_pair, c_m, b_m_t, router_w1,
                router_w2, w1, w2, w3, out):
    B, L, D = x.shape
    CH = L // STEPS
    INNER = w_in_t.shape[1] // 2
    M = INNER // P
    S = a_pair.shape[0]
    E, _, DFF = w1.shape
    FH = DFF // P
    G = 4
    NG = E // G
    HALF = STEPS // 2
    W = HALF * CH
    UNITS = 2 * B
    PART = HALF // 2
    FFN_BUFS = 3
    SLOTS = 8
    PAD = (STEPS - 1) * S
    assert CH == P and D == P and M == 2 and STEPS * S == P and G * CAPACITY == P and W == 512
    assert B == 4 and CH == 2 * STEPS * STEPS and E <= 32

    x_rows = x.rearrange("b (c j) d -> b c (j d)", j=STEPS)
    out_rows = out.rearrange("b (c j) d -> b c (j d)", j=STEPS)
    norm_rows = nc.dram_tensor("norm_rows", [B * L, D], F32, kind="Internal").ap()
    norm_by_chunk = norm_rows.rearrange("(b c j) d -> b c (j d)", b=B, j=STEPS)

    with ExitStack() as ctx:
        def sb(name, shape, dt=F32):
            return ctx.enter_context(nc.sbuf_tensor(name, shape, dt))

        def sem(name):
            return ctx.enter_context(nc.semaphore(name))

        bank = [ctx.enter_context(nc.psum_tensor(f"bank{i}", [P, W], F32)) for i in range(8)]

        ident = sb("ident", [P, P])
        ones = sb("ones", [P, P])
        minus_half = sb("minus_half", [P, STEPS])
        batch_row = sb("batch_row", [P, NG, B])
        select_last = sb("select_last", [S, P])
        vec = sb("vec", [P, vectors.shape[1]])
        cond = vec[:, 0:4]
        gamma, beta = vec[:, 4:5], vec[:, 5:6]
        conv_b = vec[:, 6:8]
        conv_w = vec[:, 8:16]
        win_t = sb("win_t", [P, 2 * INNER])
        win_x = sb("win_x", [P, M, D])
        wout_t = sb("wout_t", [P, M, D])
        apair = sb("apair", [S, 2, S])
        bm_t = sb("bm_t", [P, M, S])
        c_block = sb("c_block", [P, STEPS, INNER])
        r1 = sb("r1", [P, P])
        r2 = sb("r2", [P, 2, 2 * E])
        next_half = sb("next_half", [P, P])
        lane = sb("lane", [P, 1], I32)
        half_start = sb("half_start", [P, 1])
        experts = sb("experts", [P, SLOTS, 2 * DFF + FH * D])

        cond_s = sb("cond_s", [P, B])
        shift_a = sb("shift_a", [P, B, D])
        scale_a = sb("scale_a", [P, B, D])
        gates = sb("gates", [P, B, 2 * D])
        mod_b = sb("mod_b", [P, 2, B])
        wout_g = sb("wout_g", [P, B, M, D])

        powers = sb("powers", [S, 3, (STEPS + 1) * S])
        plain = sb("plain", [S, 3, 4, S])
        bin_w = sb("bin_w", [S, D])
        into_pad = sb("into_pad", [P, PAD + P])
        last_pad = sb("last_pad", [P, 2, PAD + P + S])
        y1 = sb("y1", [P, B, CH])
        y2 = sb("y2", [P, B, 16])
        y3 = sb("y3", [P, B, 2])
        carry2 = sb("carry2", [S, B, 16])
        carry1 = sb("carry1", [S, B, CH])

        xs = sb("xs", [P, B, STEPS, D])
        hs = sb("hs", [P, B, STEPS, D])
        xhat = sb("xhat", [P, STEPS, D])
        xn = sb("xn", [P, STEPS, D])
        xn_t = sb("xn_t", [P, 2, STEPS, CH])
        HALO = CONV_TAPS - 1
        u = sb("u", [P, M, HALO + STEPS, CH])
        conv = sb("conv", [P, M, B, STEPS * CH])
        gate_z = sb("gate_z", [P, M, B, STEPS * CH])
        y = sb("y", [P, 2, M, W])
        early = y[:, :, :, :].rearrange("p a m t -> p (a m t)")
        wmod = early[:, 0:6 * D]
        cond_rows = early[:, 6 * D:(6 + B) * D].rearrange("p (b t) -> p b t", b=B)
        gate_a_parts = gate_z[:, 0, B - 1].rearrange("p (a b t) -> p a b t", a=2, b=B)
        gate_b_parts = y[:, 0].rearrange("p a (b t) -> p a b t", b=B)
        token_of = xn_t[:, 0]
        xhat3 = sb("xhat3", [P, 2, HALF, D])
        h2_t = sb("h2_t", [P, 2, W])
        routed = xs
        st1 = sb("st1", [P, STEPS, 6])
        st2 = sb("st2", [P, STEPS, 6])
        tmp = sb("tmp", [P, 4, STEPS])
        mean_var = sb("mean_var", [P, STEPS, 2])
        neg_mean = sb("neg_mean", [P, 3, B, STEPS])
        neg_shift = sb("neg_shift", [P, 3, B, STEPS])
        var = sb("var", [P, 3, B, STEPS])
        rstd = sb("rstd", [P, 3, B, STEPS])

        left = [xn[:, k * HALF:(k + 1) * HALF, :].rearrange("p j d -> p (j d)") for k in range(2)]
        exps = xhat[:, 0:HALF, :].rearrange("p j d -> p (j d)")
        found = sb("found", [P, 2 * CAPACITY])
        found_at = sb("found_at", [P, CAPACITY], U32)
        neg_max = sb("neg_max", [P, 2])
        half_max = sb("half_max", [P, 2])
        half_sum = sb("half_sum", [P, 2])
        half_part = sb("half_part", [P, 2])
        best = sb("best", [P, CAPACITY])
        best_token = sb("best_token", [P, CAPACITY])
        keep = sb("keep", [P, CAPACITY])
        exp_all = sb("exp_all", [P, 2])
        exp_top = sb("exp_top", [P, 1])
        e_top = sb("e_top", [P, CAPACITY])
        rz = sb("rz", [P, 1])
        den = sb("den", [P, 1])
        rden = sb("rden", [P, 1])
        w_top = sb("w_top", [P, CAPACITY])
        table_call = sb("table_call", [P, 1])
        slot_at = sb("slot_at", [P, 2, NG * B])
        slot_row = sb("slot_row", [P, NG * B], U32)

        def over(base, at, dt, *shape):
            n = 1
            for d in shape:
                n *= d
            flat = base[:, :, :, :].rearrange("p m b t -> p (m b t)")
            size = 2 if dt == BF16 else 4
            ap = flat[:, at // 4:(at + n * size) // 4]
            ap = ap if dt == F32 else ap.bitcast(dt)
            names = "abcdef"[:len(shape)]
            return ap.rearrange(f"p ({' '.join(names)}) -> p {' '.join(names)}",
                                **dict(zip(names[1:], shape[1:]))), at + n * size

        onehot, _ = over(conv, 0, BF16, NG, B, STEPS * CH)
        picked, at = over(gate_z, 0, F32, NG, B, D)
        picked_t, at = over(gate_z, at, F32, 2, G, B, CAPACITY)
        silu_g, at = over(gate_z, at, F32, FFN_BUFS, FH * P)
        hidden = (xn_t[:, 1].rearrange("p (q f) t -> p q f t", q=G),
                  y[:, 1].rearrange("p m t -> p (m t)").rearrange("p (q f t) -> p q f t", q=G, f=FH))
        value, at = over(gate_z, at, F32, B, D)
        rest, at = over(gate_z, at, F32, B, D)
        parts, at = over(gate_z, at, BF16, NG, 3, B, D)

        in_x = [sem(f"in_x{b}") for b in range(B)]
        in_x0_rest = sem("in_x0_rest")
        in_vec, in_wmod, in_win, in_winx, in_wout, in_a, in_bm = (
            sem(n) for n in ("in_vec", "in_wmod", "in_win", "in_winx", "in_wout", "in_a", "in_bm"))
        in_c, in_r1, in_r2 = sem("in_c"), sem("in_r1"), sem("in_r2")
        in_expert = [sem(f"in_expert{i}") for i in range(SLOTS)]
        in_expert_out = [sem(f"in_expert_out{i}") for i in range(SLOTS)]
        const_ready = sem("const_ready")
        pool_order, dve_order = sem("pool_order"), sem("dve_order")
        ones_ready = sem("ones_ready")
        cond_ready = sem("cond_ready")
        cond_rows_ready = sem("cond_rows_ready")
        mod_mm = sem("mod_mm")
        mod_ready = sem("mod_ready")
        raw_ready = sem("raw_ready")
        gates_ready = sem("gates_ready")
        wout_ready = sem("wout_ready")
        pow_mm, pow_ready = sem("pow_mm"), sem("pow_ready")
        var_ready = sem("var_ready")
        rstd_ready = sem("rstd_ready")
        moments_ready = sem("moments_ready")
        xhat_ready = sem("xhat_ready")
        h_ready = sem("h_ready")
        xn_ready = sem("xn_ready")
        h0_ready = sem("h0_ready")
        gated_h = sem("gated_h")
        base_ready = sem("base_ready")
        tr_done, xnt_ready = sem("tr_done"), sem("xnt_ready")
        xz_mm, xz_read = sem("xz_mm"), sem("xz_read")
        scan_in = sem("scan_in")
        tap_done, conv_done = sem("tap_done"), sem("conv_done")
        silu_done = sem("silu_done")
        scan_mm, scan_step = sem("scan_mm"), sem("scan_step")
        state_ready = sem("state_ready")
        sc_mm, sc_read = sem("sc_mm"), sem("sc_read")
        y_ready = sem("y_ready")
        out_mm, x1_ready = sem("out_mm"), sem("x1_ready")
        xhat3_ready, stored = sem("xhat3_ready"), [sem("stored0"), sem("stored1")]
        tr3_done, h2_ready, router_mm, routed_ready = (
            sem("tr3_done"), sem("h2_ready"), sem("router_mm"), sem("routed_ready"))
        logits_mm = sem("logits_mm")
        left_ready, index_ready = sem("left_ready"), sem("index_ready")
        found_ready, other_mm, merged = sem("found_ready"), sem("other_mm"), sem("merged")
        max_ready, exp_ready = sem("max_ready"), sem("exp_ready")
        weights_ready = sem("weights_ready")
        slots_mm, slots_ready = sem("slots_mm"), sem("slots_ready")
        picked_first = [sem(f"picked_first{b}") for b in range(B)]
        picked_in = [None] + [sem(f"picked_in{g}") for g in range(1, NG)]
        ptr_done, pickt_ready = sem("ptr_done"), sem("pickt_ready")
        ffn_mm, silu_g_ready, hidden_ready = sem("ffn_mm"), sem("silu_g_ready"), sem("hidden_ready")
        eout_mm, value_ready = sem("eout_mm"), sem("value_ready")
        hi_ready, mid_ready, lo_ready, rest_ready = (
            sem("hi_ready"), sem("mid_ready"), sem("lo_ready"), sem("rest_ready"))
        onehot_ready = sem("onehot_ready")
        scatter_mm, final_ready = sem("scatter_mm"), sem("final_ready")
        out_stored = sem("out_stored")

        tr_bank = bank[0:2]
        xz_bank = bank[2:6]
        y_bank, small_bank = bank[6], bank[7]
        sc_bank, out_bank, tr3_bank, router_bank = bank[2:4], bank[4], (bank[0], bank[7]), (bank[1], bank[6])
        logit_bank, other_bank = bank[5], bank[6]
        ptr_bank, slot_bank, ffn_bank, eout_bank = bank[0], (bank[1], bank[7]), bank[1:4], bank[4]
        ptr_first = (bank[0], bank[4], bank[5], bank[6])
        scatter_bank = bank[5:8] + bank[1:4] + [bank[0], bank[4]]
        last_banks = (scatter_bank[UNITS - 1], scatter_bank[0])

        FIRST_RSTD = [1, 2, 4, 6]
        SECOND_RSTD = [3, 5, 7, 8]
        FIRST_VAR = [1, 2, 4, 5]
        SECOND_VAR = 3
        H_READY = [[1, None]] + [[2 * b, 2 * b + 1] for b in range(1, B)]

        POW = (0, 5, 8)

        block = ctx.enter_context(nc.Block())

        @block.sync
        def _(sp):
            sp.dma_start(vec[:, :], vectors).then_inc(in_vec, 16)
            for hf in range(2):
                sp.dma_start(xs[:, 0, hf * HALF:(hf + 1) * HALF].rearrange("p j d -> p (j d)"),
                             x_rows[0][:, hf * W:(hf + 1) * W]).then_inc(in_x[0] if hf == 0 else in_x0_rest, 16)
            sp.dma_start(wmod[:, :], w_mod).then_inc(in_wmod, 16)
            sp.dma_start(apair[:, :, :], a_pair).then_inc(in_a, 16)
            for b in (1, 2):
                sp.dma_start(xs[:, b], x_rows[b]).then_inc(in_x[b], 16)
            sp.dma_start(win_t[:, :], w_in_t).then_inc(in_win, 16)
            sp.dma_start(bm_t[:, :, :], b_m_t).then_inc(in_bm, 16)
            sp.dma_start(win_x[:, :, :], w_in_x).then_inc(in_winx, 16)
            sp.dma_start(xs[:, 3], x_rows[3]).then_inc(in_x[3], 16)
            sp.dma_start(wout_t[:, :, :], w_out_t).then_inc(in_wout, 16)
            sp.dma_start(r1[:, :], router_w1).then_inc(in_r1, 16)
            sp.wait_ge(const_ready, 4)
            for j in range(STEPS):
                sp.dma_start(c_block[S * j:S * (j + 1), j, :], c_m).then_inc(in_c, 16)
            sp.dma_start(r2[:, 0, 0:E], router_w2).then_inc(in_r2, 16)
            sp.dma_start(r2[:, 1, E:2 * E], router_w2).then_inc(in_r2, 16)

            def load_expert_in(e):
                s = e % SLOTS
                if e >= SLOTS:
                    sp.wait_ge(ffn_mm, e - SLOTS + 1)
                sp.dma_start(experts[:, s, 0:DFF], w1[e]).then_inc(in_expert[s], 16)
                sp.dma_start(experts[:, s, DFF:2 * DFF], w2[e]).then_inc(in_expert[s], 16)

            def load_expert_out(e):
                s = e % SLOTS
                if e >= SLOTS and e % G == 0:
                    sp.wait_ge(eout_mm, (e - SLOTS) // G + 1)
                sp.dma_start(experts[:, s, 2 * DFF:].rearrange("p (f d) -> p f d", f=FH), w3[e]).then_inc(
                    in_expert_out[s], 16)

            for e in range(SLOTS):
                load_expert_in(e)
                load_expert_out(e)
            with sp.Fori(0, B) as b:
                for hf in range(2):
                    sp.wait_ge(xhat3_ready, 2 * b + hf + 1)
                    sp.dma_start(norm_by_chunk[b][:, hf * W:(hf + 1) * W],
                                 xhat3[:, hf].rearrange("p j d -> p (j d)")).then_inc(stored[hf], 16)
            for g in range(SLOTS // G, NG):
                for e in range(G * g, G * (g + 1)):
                    load_expert_in(e)
                for e in range(G * g, G * (g + 1)):
                    load_expert_out(e)
            def store(b, j0, n):
                sp.dma_start(out_rows[b][:, j0 * D:(j0 + n) * D],
                             hs[:, b, j0:j0 + n, :].rearrange("p j d -> p (j d)")).then_inc(out_stored, 16)

            with sp.Fori(0, B - 1) as b:
                for hf in range(2):
                    sp.wait_ge(final_ready, 2 * b + hf + 1)
                    store(b, hf * HALF, HALF)
            sp.wait_ge(final_ready, UNITS - 1)
            store(B - 1, 0, HALF)
            for part in range(2):
                sp.wait_ge(final_ready, UNITS + part)
                store(B - 1, HALF + part * PART, PART)
            sp.wait_ge(out_stored, 16 * (UNITS + 1))

        @block.gpsimd
        def _(pool):
            order = Order(pool, pool_order)
            order.after(pool.memset(ident[:, :], 0.0))
            pool.affine_select(out=ident[:, :], in_=ident[:, :], compare_op=ALU.not_equal, fill=1.0, base=0,
                               pattern=[[-1, P]], channel_multiplier=1).then_inc(const_ready, 1)
            pool.memset(minus_half[:, :], -0.5).then_inc(const_ready, 1)

            def power(kind, b, j0, n, count=None):
                if count is not None:
                    pool.wait_ge(var_ready, count)
                r = rstd[:, kind, b, j0:j0 + n]
                ins = pool.tensor_tensor(r, var[:, kind, b, j0:j0 + n], minus_half[:, 0:n], ALU.pow)
                if kind != 1:
                    order.after(ins)
                    ins = pool.tensor_tensor(neg_shift[:, kind, b, j0:j0 + n], neg_mean[:, kind, b, j0:j0 + n], r,
                                             ALU.mult)
                ins.then_inc(rstd_ready, 1)

            pool.memset(r2[:, :, :], 0.0).then_inc(const_ready, 1)
            pool.memset(c_block[:, :, :], 0.0).then_inc(const_ready, 1)
            pool.wait_ge(const_ready, 2)
            power(0, 0, 0, STEPS, FIRST_VAR[0])
            pool.memset(into_pad[:, 0:PAD], 0.0).then_inc(const_ready, 1)
            pool.memset(last_pad[:, :, 0:PAD], 0.0).then_inc(const_ready, 1)
            order.after(pool.memset(select_last[:, :], 0.0))
            pool.affine_select(out=select_last[:, :], in_=select_last[:, :], compare_op=ALU.not_equal,
                               fill=1.0, base=PAD, pattern=[[-1, P]], channel_multiplier=1
                               ).then_inc(const_ready, 1)
            pool.memset(u[:, :, 0:HALO, 0:1], 0.0).then_inc(const_ready, 1)
            pool.memset(carry2[:, :, 0:1], 0.0).then_inc(const_ready, 1)
            pool.memset(carry1[:, :, 0:1], 0.0).then_inc(const_ready, 1)

            def spread(b):
                pool.wait_ge(moments_ready, b)
                mu_e, mu_o, m2_e, m2_o = (st2[:, :, k] for k in (1, 4, 2, 5))
                total, gap, m2, gap2 = (tmp[:, k, :] for k in range(4))
                pool.tensor_tensor(gap, mu_e, mu_o, ALU.subtract)
                pool.tensor_tensor(total, mu_e, mu_o, ALU.add)
                order.after(pool.tensor_tensor(m2, m2_e, m2_o, ALU.add))
                pool.tensor_scalar(gap, gap, 0.5, None, ALU.mult)
                pool.tensor_scalar(m2, m2, 1.0 / D, LN_EPS, ALU.mult, ALU.add)
                order.after(pool.tensor_scalar(neg_mean[:, 1, b, :], total, -0.5, None, ALU.mult))
                order.after(pool.tensor_tensor(gap2, gap, gap, ALU.mult))
                order.after(pool.tensor_tensor(var[:, 1, b, :], gap2, m2, ALU.add))

            def per_row(table, b, n):
                return table[:, b, 0:D].unsqueeze(1).to_broadcast([P, n, D])

            def modulated(b):
                pool.wait_ge(mod_ready, b + 1)
                for hf in range(1 if b == 0 else 2):
                    pool.wait_ge(xhat_ready, H_READY[b][hf])
                    tiles = slice(hf * HALF, (hf + 1) * HALF)
                    order.after(pool.tensor_tensor(hs[:, b, tiles], xhat[:, tiles, :], per_row(scale_a, b, HALF),
                                                   ALU.mult))
                    pool.tensor_tensor(hs[:, b, tiles], hs[:, b, tiles], per_row(shift_a, b, HALF), ALU.add
                                       ).then_inc(h_ready, 1)

            def base(b):
                pool.wait_ge(xn_ready, 2 * b + 2)
                pool.tensor_tensor(hs[:, b], hs[:, b], per_row(gates, b, STEPS), ALU.mult).then_inc(gated_h, 1)
                pool.wait_ge(gated_h, b + 1)
                pool.tensor_tensor(hs[:, b], hs[:, b], xs[:, b], ALU.add).then_inc(base_ready, 1)

            modulated(0)
            power(0, 1, 0, STEPS, FIRST_VAR[1])
            power(1, 0, 0, STEPS, SECOND_VAR)
            modulated(1)
            power(0, 2, 0, STEPS, FIRST_VAR[2])
            for b in range(1, B):
                spread(b)
                power(1, b, 0, STEPS)
                if b == 1:
                    power(0, 3, 0, STEPS, FIRST_VAR[3])
                if b + 1 < B:
                    modulated(b + 1)
            pool.wait_ge(gates_ready, 1)
            with pool.Fori(0, B) as b:
                base(b)

            def third_power(n):
                b, j0 = n // 2, (n % 2) * HALF
                pool.wait_ge(moments_ready, B + n)
                pool.tensor_scalar(neg_mean[:, 2, b, j0:j0 + HALF], mean_var[:, j0:j0 + HALF, 0], -1.0, None, ALU.mult)
                order.after(pool.tensor_scalar(var[:, 2, b, j0:j0 + HALF], mean_var[:, j0:j0 + HALF, 1], LN_EPS, None,
                                               ALU.add))
                power(2, b, j0, HALF)

            third_power(0)
            third_power(1)
            pool.wait_ge(xz_mm, 8 * B)
            pool.iota(token_of[:, :, :], pattern=[[1, STEPS], [STEPS, CH]], base=0, channel_multiplier=0,
                      allow_small_or_imprecise_dtypes=True).then_inc(const_ready, 1)
            pool.iota(batch_row[:, :, :], pattern=[[0, NG], [L, B]], base=0, channel_multiplier=0,
                      allow_small_or_imprecise_dtypes=True).then_inc(const_ready, 1)
            pool.iota(lane[:, :], pattern=[[0, 1]], base=0, channel_multiplier=1).then_inc(const_ready, 1)
            order.after(pool.memset(next_half[:, :], 0.0))
            pool.affine_select(out=next_half[:, :], in_=next_half[:, :], compare_op=ALU.not_equal,
                               fill=1.0, base=-E, pattern=[[-1, P]], channel_multiplier=1
                               ).then_inc(const_ready, 1)
            for n in range(2, UNITS):
                third_power(n)

            pool.wait_ge(slots_ready, 1)
            pool.wait_ge(stored[0], 16 * B)
            pool.wait_ge(stored[1], 16 * B)
            for t in range(NG * B):
                pool.indirect_dma_start(
                    out=picked[:, t // B, t % B, :], out_offset=None, in_=norm_rows,
                    in_offset=bass.IndirectOffsetOnAxis(ap=slot_row[:, t:t + 1], axis=0),
                ).then_inc(picked_first[t] if t < B else picked_in[t // B], 16)
            with pool.Fori(0, NG) as g:
                pool.wait_ge(hi_ready, g + 1)
                pool.tensor_tensor(rest, value, parts[:, g, 0], ALU.subtract).then_inc(rest_ready, 1)
                pool.wait_ge(mid_ready, g + 1)
                pool.tensor_tensor(rest, rest, parts[:, g, 1], ALU.subtract).then_inc(rest_ready, 1)

        @block.scalar
        def _(act):
            def norm(kind, dst, src, b, j0, n, ready):
                act.wait_ge(rstd_ready, ready)
                for j in range(n):
                    ins = act.activation(dst(j), src(j), ACT.Identity, scale=rstd[:, kind, b, j0 + j:j0 + j + 1],
                                         bias=neg_shift[:, kind, b, j0 + j:j0 + j + 1])
                return ins

            def first_norm(b, hf):
                if b == 1 and hf == 1:
                    act.wait_ge(h0_ready, 1)
                elif b > 0:
                    act.wait_ge(h_ready, H_READY[b - 1][hf])
                norm(0, lambda j: xhat[:, hf * HALF + j, :], lambda j: xs[:, b, hf * HALF + j, :], b, hf * HALF,
                     HALF, FIRST_RSTD[b]).then_inc(xhat_ready, 1)

            def transposed(b):
                for hf in range(2):
                    act.wait_ge(tr_done, 2 * b + hf + 1)
                    if b > 1:
                        act.wait_ge(xz_mm, 8 * (b - 1))
                    act.activation(xn_t[:, b % 2, hf * HALF:(hf + 1) * HALF, :], tr_bank[hf][:, :],
                                   ACT.Identity, scale=gamma, bias=beta).then_inc(xnt_ready, 1)

            def silu_conv(b, m):
                act.wait_ge(conv_done, 2 * b + m + 1)
                act.activation(conv[:, m, b], conv[:, m, b], ACT.Silu).then_inc(silu_done, 1)

            def power_step(r, k):
                n = 1 << k
                act.wait_ge(pow_mm, POW[r] + k + 1)
                ins = act.activation(powers[:, r, (n + 1) * S:(2 * n + 1) * S], small_bank[0:S, 0:n * S], ACT.Copy)
                if n == 4 and r < 2:
                    act.activation(powers[:, r + 1, S:2 * S], small_bank[0:S, 3 * S:4 * S], ACT.Copy)
                    ins = act.activation(plain[:, r + 1, 0, :], small_bank[0:S, 4 * S:5 * S], ACT.Copy)
                elif n < 4:
                    ins = act.activation(plain[:, r, k + 1, :], small_bank[0:S, n * S:(n + 1) * S], ACT.Copy)
                ins.then_inc(pow_ready, 1)

            act.wait_ge(in_vec, 16)
            act.activation(cond_s[:, :], cond, ACT.Silu).then_inc(cond_ready, 1)
            for b in range(B):
                if b == 1:
                    first_norm(0, 0)
                act.wait_ge(mod_mm, b + 1)
                act.activation(scale_a[:, b, :], xz_bank[b][:, D:2 * D], ACT.Identity, bias=1.0)
                act.activation(shift_a[:, b, :], xz_bank[b][:, 0:D], ACT.Copy).then_inc(mod_ready, 1)
                act.activation(gates[:, b, :], xz_bank[b][:, 2 * D:4 * D], ACT.Copy).then_inc(raw_ready, 1)
            act.wait_ge(mod_mm, B + 1)
            act.activation(mod_b[:, 0, :], small_bank[:, 0:B], ACT.Copy)
            act.activation(mod_b[:, 1, :], small_bank[:, B:2 * B], ACT.Identity, bias=1.0
                           ).then_inc(mod_ready, 1)
            act.wait_ge(const_ready, 1)
            act.wait_ge(in_a, 16)
            for r in range(3):
                act.activation(powers[:, r, 0:S], ident[0:S, 0:S], ACT.Copy)
            act.activation(powers[:, 0, S:2 * S], apair[:, 1, :], ACT.Copy)
            act.activation(plain[:, 0, 0, :], apair[:, 0, :], ACT.Copy).then_inc(pow_ready, 1)
            for k in range(3):
                power_step(0, k)
            first_norm(1, 0)
            first_norm(1, 1)
            act.wait_ge(pow_mm, 4)
            act.activation(bin_w[:, :], small_bank[0:S, 0:D], ACT.Copy).then_inc(pow_ready, 1)
            act.wait_ge(pow_mm, 5)
            act.activation(into_pad[:, PAD:], small_bank[:, 0:P], ACT.Copy).then_inc(pow_ready, 1)

            transposed(0)
            for b in range(B):
                n = 8 * b
                for m in range(M):
                    for hf in range(2):
                        n += 1
                        act.wait_ge(xz_mm, n)
                        if b == 0:
                            act.wait_ge(const_ready, 8)
                        else:
                            act.wait_ge(conv_done, 2 * (b - 1) + m + 1)
                        src = xz_bank[(n - 1) % 4]
                        tiles = src[:, :].rearrange("p (j c) -> p j c", c=CH)
                        act.activation(u[:, m, HALO + hf * HALF:HALO + (hf + 1) * HALF, :], tiles, ACT.Copy)
                        if hf == 1:
                            act.activation(u[:, m, 0:HALO, 1:], tiles[:, HALF - HALO:, 0:CH - 1], ACT.Copy)
                        act.activation(conv[:, m, b, hf * W:(hf + 1) * W], src[:, :], ACT.Identity,
                                       scale=conv_w[:, CONV_TAPS * (m + 1) - 1:CONV_TAPS * (m + 1)],
                                       bias=conv_b[:, m:m + 1]).then_inc(xz_read, 1)
                        if b in (1, 2) and m + hf == 1:
                            power_step(b, m)
                    if b + 2 < B:
                        first_norm(b + 2, m)
                for k in range(2 * M):
                    hf, m = k // M, k % M
                    n += 1
                    act.wait_ge(xz_mm, n)
                    act.activation(gate_z[:, m, b, hf * W:(hf + 1) * W], xz_bank[(n - 1) % 4][:, :],
                                   ACT.Tanh, scale=0.5).then_inc(xz_read, 1)
                    if b in (1, 2) and k == 0:
                        power_step(b, 2)
                    if b == 2 and k == 2:
                        act.wait_ge(pow_mm, 12)
                        act.activation(last_pad[:, :, PAD:], small_bank[:, 0:2 * (P + S)].rearrange(
                            "p (r t) -> p r t", r=2), ACT.Copy).then_inc(pow_ready, 1)
                    if b + 1 < B and k == 1:
                        transposed(b + 1)
                    if b == B - 1:
                        silu_conv(k // M, k % M)
            with act.Fori(2, B) as b:
                for m in range(M):
                    silu_conv(b, m)

            def third_norm(k):
                b, hf = k // 2, k % 2
                if k >= 2:
                    act.wait_ge(tr3_done, k - 1)
                    act.wait_ge(stored[hf], 16 * (k // 2))
                norm(2, lambda j: xhat3[:, hf, j, :], lambda j: hs[:, b, hf * HALF + j, :], b, hf * HALF, HALF,
                     2 * B + k + 1).then_inc(xhat3_ready, 1)

            def second_modulation(k):
                b, hf = k // 2, k % 2
                act.wait_ge(tr3_done, k + 1)
                if k >= 2:
                    act.wait_ge(router_mm, k - 1)
                act.activation(h2_t[:, hf, :], tr3_bank[hf][:, :], ACT.Identity, scale=mod_b[:, 1, b:b + 1],
                               bias=mod_b[:, 0, b:b + 1]).then_inc(h2_ready, 1)

            def router_silu(k):
                b, hf = k // 2, k % 2
                act.wait_ge(router_mm, k + 1)
                act.wait_ge(base_ready, B)
                act.activation(routed[:, b, hf * HALF:(hf + 1) * HALF, :],
                               router_bank[hf][:, :].rearrange("p (j c) -> p j c", c=CH), ACT.Silu
                               ).then_inc(routed_ready, 1)

            for n in range(1, UNITS):
                if n >= 4:
                    router_silu(n - 4)
                if n >= 3:
                    second_modulation(n - 3)
                third_norm(n - 1)
            second_modulation(UNITS - 3)
            router_silu(UNITS - 4)
            third_norm(UNITS - 1)
            second_modulation(UNITS - 2)
            router_silu(UNITS - 3)
            second_modulation(UNITS - 1)
            router_silu(UNITS - 2)
            router_silu(UNITS - 1)
            act.wait_ge(max_ready, 1)
            act.wait_ge(index_ready, 1)
            act.activation(exps, logit_bank[:, :], ACT.Exp, bias=neg_max[:, 0:1],
                           accum_out=half_sum[:, 0:1]).then_inc(exp_ready, 1)
            act.wait_ge(max_ready, 2)
            act.activation(e_top[:, :], best[:, :], ACT.Exp, bias=neg_max[:, 1:2], accum_out=exp_top[:, 0:1])
            act.activation(half_part[:, :], half_max[:, :], ACT.Exp, bias=neg_max[:, 1:2]).then_inc(exp_ready, 1)
            act.activation(table_call[:, :], cond_s[:, 0:1], ACT.Silu)

            def chosen_norm(g):
                if g > 0:
                    act.wait_ge(ptr_done, B + g)
                if g >= 2:
                    act.wait_ge(ffn_mm, G * (g - 1))
                for b in range(B):
                    if g == 0:
                        act.wait_ge(ptr_done, b + 1)
                        src = ptr_first[b][:, 0:P]
                    else:
                        src = ptr_bank[:, b * P:(b + 1) * P]
                    ins = act.activation(picked_t[:, g % 2, :, b, :], src.rearrange("p (q c) -> p q c", q=G),
                                         ACT.Identity, scale=mod_b[:, 1, b:b + 1], bias=mod_b[:, 0, b:b + 1])
                ins.then_inc(pickt_ready, 1)

            def part(g, i):
                if i == 0:
                    act.wait_ge(value_ready, g + 1)
                    act.activation(parts[:, g, 0], value, ACT.Copy).then_inc(hi_ready, 1)
                elif i == 1:
                    act.wait_ge(rest_ready, 2 * g + 1)
                    act.activation(parts[:, g, 1], rest, ACT.Copy).then_inc(mid_ready, 1)
                else:
                    act.wait_ge(rest_ready, 2 * g + 2)
                    act.activation(parts[:, g, 2], rest, ACT.Copy).then_inc(lo_ready, 1)

            chosen_norm(0)
            for e in range(E):
                g, q = e // G, e % G
                act.wait_ge(ffn_mm, e + 1)
                if e >= FFN_BUFS:
                    act.wait_ge(hidden_ready, e - FFN_BUFS + 1)
                act.activation(silu_g[:, e % FFN_BUFS, :], ffn_bank[e % FFN_BUFS][:, 0:FH * P], ACT.Silu
                               ).then_inc(silu_g_ready, 1)
                if g >= 1 and q == G - 1:
                    part(g - 1, 0)
                if g >= 2 and q < 2:
                    part(g - 2, q + 1)
                if q == 1 and g + 1 < NG:
                    chosen_norm(g + 1)
            part(NG - 2, 1)
            part(NG - 2, 2)
            for i in range(3):
                part(NG - 1, i)

        @block.tensor
        def _(pe):
            def unread(dest, n):
                pe.matmul(dest[:, 0:n], ident[:, :], win_t[:, 0:n], start=True, stop=True)

            pe.wait_ge(in_wmod, 16)
            for b in range(B):
                pe.wait_ge(cond_rows_ready, b + 1)
                pe.matmul(xz_bank[b][:, 0:3 * D], cond_rows[:, b, :], wmod[:, 0:3 * D], start=True, stop=True)
                pe.matmul(xz_bank[b][:, 3 * D:4 * D], cond_rows[:, b, :], wmod[:, 5 * D:6 * D], start=True,
                          stop=True).then_inc(mod_mm, 1)
            pe.matmul(small_bank[:, 0:B], wmod[:, 3 * D:4 * D], cond_s[:, :], start=True, stop=True)
            pe.matmul(small_bank[:, B:2 * B], wmod[:, 4 * D:5 * D], cond_s[:, :], start=True, stop=True
                      ).then_inc(mod_mm, 1)

            def power_product(r, k):
                tb, n = powers[:, r, :], 1 << k
                pe.wait_ge(pow_ready, POW[r] + k + 1)
                pe.matmul(small_bank[0:S, 0:n * S], plain[:, r, k, :], tb[:, S:(n + 1) * S], start=True, stop=True)
                pe.matmul(small_bank[0:S, n * S:(n + 1) * S], tb[:, n * S:(n + 1) * S], plain[:, r, k, :],
                          start=True, stop=True).then_inc(pow_mm, 1)

            for k in range(3):
                power_product(0, k)
            pe.wait_ge(in_bm, 16)
            pe.wait_ge(in_winx, 16)
            pe.wait_ge(pow_ready, 4)
            for m in range(M):
                ins = pe.matmul(small_bank[0:S, 0:D], bm_t[:, m, :], win_x[:, m, :], start=(m == 0),
                                stop=(m == M - 1))
            ins.then_inc(pow_mm, 1)
            pe.wait_ge(in_win, 16)
            unread(y_bank, W)
            unread(y_bank, W)
            pe.wait_ge(pow_ready, 5)
            pe.matmul(small_bank[:, 0:P], bin_w[:, :], powers[:, 0, 0:P], start=True, stop=True).then_inc(pow_mm, 1)

            y1v = y1[:, :, :].rearrange("p b (C i) -> p b C i", i=STEPS)
            y2v = y2[:, :, :].rearrange("p b (g i) -> p b g i", i=STEPS)
            c2 = small_bank[0:S, 128:128 + 16 * B].rearrange("p (b C) -> p b C", b=B)
            c1 = tr_bank[0][0:S, :].rearrange("p (b C) -> p b C", b=B)

            def scan_product(k):
                pe.wait_ge(scan_step, k + 1)
                if k == 0:
                    pe.wait_ge(pow_ready, 13)
                    pe.wait_ge(const_ready, 6)
                    for i in range(STEPS):
                        ins = pe.matmul(small_bank[:, 0:B * 16], last_pad[:, 0, PAD - S * i:PAD - S * i + P],
                                        y1v[:, :, :, i], start=(i == 0), stop=(i == STEPS - 1))
                elif k == 1:
                    for i in range(STEPS):
                        ins = pe.matmul(small_bank[:, 64:64 + 2 * B], last_pad[:, 1, PAD - S * i:PAD - S * i + P],
                                        y2v[:, :, :, i], start=(i == 0), stop=(i == STEPS - 1))
                elif k == 2:
                    ins = pe.matmul(small_bank[:, 76:76 + B], last_pad[:, 1, PAD + S:PAD + S + P], y3[:, :, 0],
                                    start=True, stop=True)
                elif k == 3:
                    for i in range(STEPS):
                        n = 2 if i < STEPS - 1 else 1
                        ins = pe.matmul(c2[:, :, i + 1:i + 1 + STEPS * (n - 1) + 1:STEPS],
                                        ident[:, S * i:S * (i + 1)], y3[:, :, 0:n], start=True, stop=True)
                elif k == 4:
                    ins = pe.matmul(small_bank[:, 192:192 + 16 * B], powers[:, 1, S:],
                                    carry2[:, :, :].rearrange("p b C -> p (b C)"), start=True, stop=True)
                elif k == 5:
                    for i in range(STEPS):
                        n = 16 if i < STEPS - 1 else 15
                        ins = pe.matmul(c1[:, :, i + 1:i + 1 + STEPS * (n - 1) + 1:STEPS],
                                        ident[:, S * i:S * (i + 1)], y2[:, :, 0:n], start=True, stop=True)
                else:
                    ins = pe.matmul(tr_bank[1][:, :], powers[:, 0, S:], carry1[:, :, :].rearrange("p b C -> p (b C)"),
                                    start=True, stop=True)
                ins.then_inc(scan_mm, 1)

            pe.wait_ge(in_win, 16)
            for b in range(B):
                for hf in range(2):
                    pe.wait_ge(xn_ready, 2 * b + hf + 1)
                    if b > 0:
                        pe.wait_ge(xnt_ready, 2 * (b - 1) + hf + 1)
                    for k in range(HALF):
                        ins = pe.transpose(tr_bank[hf][:, k * P:(k + 1) * P], xn[:, hf * HALF + k, :],
                                           ident[:, :])
                    ins.then_inc(tr_done, 1)
                n = 8 * b

                def take_bank(n):
                    if n >= 4:
                        pe.wait_ge(xz_read, n - 3)
                    elif n == 0:
                        pe.wait_ge(raw_ready, B)
                    return xz_bank[n % 4]

                def x_part(m, hf):
                    pe.wait_ge(xnt_ready, 2 * b + hf + 1)
                    pe.matmul(take_bank(n)[:, :], win_t[:, m * P:(m + 1) * P],
                              xn_t[:, b % 2, hf * HALF:(hf + 1) * HALF, :], start=True, stop=True
                              ).then_inc(xz_mm, 1)

                x_part(0, 0)
                n += 1
                x_part(0, 1)
                n += 1
                if b in (1, 2):
                    power_product(b, 0)
                if b == 0:
                    pe.wait_ge(pow_ready, 6)
                    pe.wait_ge(const_ready, 5)
                for i in range(STEPS):
                    ins = pe.matmul(y_bank[:, b * CH:(b + 1) * CH], into_pad[:, PAD - S * i:PAD - S * i + P],
                                    xn_t[:, b % 2, i, :], start=(i == 0), stop=(i == STEPS - 1))
                ins.then_inc(scan_in, 1)
                for hf in range(2):
                    x_part(1, hf)
                    n += 1
                    if b in (1, 2) and hf == 0:
                        power_product(b, 1)
                    if b == B - 1:
                        scan_product(hf)
                for k in range(2 * M):
                    hf, m = k // M, k % M
                    pe.matmul(take_bank(n)[:, :], win_t[:, INNER + m * P:INNER + (m + 1) * P],
                              xn_t[:, b % 2, hf * HALF:(hf + 1) * HALF, :], start=True, stop=True
                              ).then_inc(xz_mm, 1)
                    n += 1
                    if b in (1, 2) and k == 0:
                        power_product(b, 2)
                    if b == 2 and k == 2:
                        pe.wait_ge(pow_ready, 12)
                        pe.wait_ge(const_ready, 7)
                        for r in (1, 2):
                            ins = pe.matmul(small_bank[:, (r - 1) * (P + S):r * (P + S)], select_last[:, :],
                                            powers[:, r, :], start=True, stop=True)
                        ins.then_inc(pow_mm, 1)
                    if b == B - 1:
                        scan_product((2, 3, 5, 6)[k])
                        if k == 1:
                            scan_product(4)

            pe.wait_ge(in_c, 16 * STEPS)
            pe.wait_ge(xz_read, 8 * B - 2)

            def logits_of(batches):
                for h in range(2):
                    for b in batches:
                        ins = pe.matmul(logit_bank[32 * b:32 * b + 32, :], r2[:, h, :],
                                        routed[:, b, :, h * (CH // 2):(h + 1) * (CH // 2)].rearrange("p j c -> p c j"),
                                        start=(h == 0), stop=(h == 1))
                return ins

            def normalised(k):
                pe.wait_ge(xhat3_ready, k + 1)
                if k >= 2:
                    pe.wait_ge(h2_ready, k - 1)
                for j in range(HALF):
                    ins = pe.transpose(tr3_bank[k % 2][:, j * P:(j + 1) * P], xhat3[:, k % 2, j, :], ident[:, :])
                ins.then_inc(tr3_done, 1)

            def router(k):
                pe.wait_ge(h2_ready, k + 1)
                pe.wait_ge(in_r1, 16)
                if k >= 2:
                    pe.wait_ge(routed_ready, k - 1)
                pe.matmul(router_bank[k % 2][:, :], r1[:, :], h2_t[:, k % 2, :], start=True, stop=True
                          ).then_inc(router_mm, 1)

            for n in range(UNITS + 1):
                if n < UNITS:
                    b, hf = n // 2, n % 2
                    if n == 0:
                        pe.wait_ge(state_ready, 1)
                    for m in range(M):
                        if n > 0:
                            pe.wait_ge(sc_read, 2 * n + m - 1)
                        for k in range(HALF):
                            ins = pe.matmul(sc_bank[m][:, k * CH:(k + 1) * CH],
                                            c_block[:, hf * HALF + k, m * P:(m + 1) * P], y1[:, b, :],
                                            start=True, stop=True)
                        ins.then_inc(sc_mm, 1)
                if n >= 1:
                    k1 = n - 1
                    b = k1 // 2
                    pe.wait_ge(y_ready, 2 * (k1 + 1))
                    pe.wait_ge(wout_ready, B)
                    if k1 >= 1:
                        pe.wait_ge(x1_ready, k1)
                    else:
                        pe.wait_ge(xz_read, 8 * B)
                    for k in range(HALF):
                        for m in range(M):
                            ins = pe.matmul(out_bank[:, k * D:(k + 1) * D], y[:, k1 % 2, m, k * P:(k + 1) * P],
                                            wout_g[:, b, m, :], start=(m == 0), stop=(m == M - 1))
                    ins.then_inc(out_mm, 1)
                if n >= 4:
                    router(n - 4)
                if n >= 3:
                    normalised(n - 3)
            pe.wait_ge(in_r2, 32)
            pe.wait_ge(routed_ready, UNITS // 2)
            logits_of(range(B // 2))
            normalised(UNITS - 2)
            router(UNITS - 3)
            normalised(UNITS - 1)
            router(UNITS - 2)
            router(UNITS - 1)
            pe.wait_ge(routed_ready, UNITS)
            logits_of(range(B // 2, B)).then_inc(logits_mm, 1)
            pe.wait_ge(const_ready, 14)
            pe.wait_ge(found_ready, 1)
            pe.matmul(other_bank[:, 0:2 * CAPACITY], next_half[:, :], found[:, :], start=True, stop=True
                      ).then_inc(other_mm, 1)
            pick = ident[:, :].rearrange("p (b r q) -> p q r b", b=B, q=G)
            for what, src in enumerate((best_token, w_top)):
                pe.wait_ge(weights_ready, what + 1)
                for q in range(G):
                    ins = pe.matmul(slot_bank[what][32 * q:32 * q + 32, 0:NG * B], src[:, :],
                                    pick[:, q, 0:NG, :], start=True, stop=True)
                ins.then_inc(slots_mm, 1)
                if what == 0:
                    pe.wait_ge(exp_ready, 1)
                    pe.wait_ge(merged, 1)
                    pe.matmul(other_bank[:, 2 * CAPACITY:2 * CAPACITY + 1], next_half[:, :], half_sum[:, 0:1],
                              start=True, stop=True).then_inc(other_mm, 1)

            def pick_transposes(g):
                pe.wait_ge(picked_in[g], 16 * B)
                pe.wait_ge(pickt_ready, g)
                for b in range(B):
                    ins = pe.transpose(ptr_bank[:, b * P:(b + 1) * P], picked[:, g, b, :], ident[:, :])
                ins.then_inc(ptr_done, 1)

            def first_transposes():
                unread(ffn_bank[1], W)
                for b in range(B):
                    pe.wait_ge(picked_first[b], 16)
                    pe.transpose(ptr_first[b][:, 0:P], picked[:, 0, b, :], ident[:, :]).then_inc(ptr_done, 1)
                    if b % 2 == 1:
                        unread(ffn_bank[1], W // 2)

            def expert_out(g):
                pe.wait_ge(hidden_ready, G * (g + 1))
                for q in range(G):
                    s = (g * G + q) % SLOTS
                    pe.wait_ge(in_expert_out[s], 16 * ((g * G + q) // SLOTS + 1))
                if g >= 1:
                    pe.wait_ge(value_ready, g)
                for b in range(B):
                    for f in range(FH):
                        for q in range(G):
                            s = (g * G + q) % SLOTS
                            w3_s = experts[:, s, 2 * DFF + f * D:2 * DFF + (f + 1) * D]
                            ins = pe.matmul(eout_bank[32 * q:32 * q + 32, b * D:(b + 1) * D],
                                            hidden[g % 2][:, q, f, b * CAPACITY:(b + 1) * CAPACITY], w3_s,
                                            start=(f == 0), stop=(f == FH - 1))
                ins.then_inc(eout_mm, 1)

            def scatter(n, g, dest=None, tiles=range(HALF)):
                b, hf = n // 2, n % 2
                dest = dest or scatter_bank[n]
                pe.wait_ge(onehot_ready, B * (g + 1))
                pe.wait_ge(lo_ready, g + 1)
                for k in tiles:
                    j = hf * HALF + k
                    for i in range(3):
                        ins = pe.matmul(dest[:, k * D:(k + 1) * D],
                                        onehot[:, g, b, j * CH:(j + 1) * CH], parts[:, g, i, b, :],
                                        start=(g == 0 and k == tiles[0] and i == 0),
                                        stop=(g == NG - 1 and k == tiles[-1] and i == 2))
                return ins

            EARLY, AHEAD = 3, 6
            first_transposes()
            for e in range(E):
                g, q, s = e // G, e % G, e % SLOTS
                pe.wait_ge(in_expert[s], 32 * (e // SLOTS + 1))
                pe.wait_ge(pickt_ready, g + 1)
                if e == 0:
                    pe.wait_ge(slots_ready, 2)
                if e >= FFN_BUFS:
                    pe.wait_ge(hidden_ready, e - FFN_BUFS + 1)
                for half in range(2):
                    for f in range(FH):
                        at = half * DFF + f * P
                        ins = pe.matmul(ffn_bank[e % FFN_BUFS][:, (half * FH + f) * P:(half * FH + f + 1) * P],
                                        experts[:, s, at:at + P], picked_t[:, g % 2, q], start=True,
                                        stop=True)
                ins.then_inc(ffn_mm, 1)
                if q == 1:
                    if g + 1 < NG:
                        pick_transposes(g + 1)
                    if g >= 1:
                        expert_out(g - 1)
                if q == G - 1 and g >= 2:
                    for n in range(EARLY):
                        scatter(n, g - 2)
            expert_out(NG - 1)

            pe.wait_ge(hidden_ready, E)
            for n in range(EARLY, AHEAD):
                for g in range(NG - 2):
                    scatter(n, g)
            for n in range(AHEAD):
                scatter(n, NG - 2)
            for n in range(AHEAD):
                scatter(n, NG - 1).then_inc(scatter_mm, 1)
            pe.wait_ge(value_ready, NG)
            for n in range(AHEAD, UNITS - 1):
                for g in range(NG):
                    ins = scatter(n, g)
                ins.then_inc(scatter_mm, 1)
            for part, dest in enumerate(last_banks):
                if part == 1:
                    pe.wait_ge(final_ready, 1)
                for g in range(NG):
                    ins = scatter(UNITS - 1, g, dest, range(part * PART, (part + 1) * PART))
                ins.then_inc(scatter_mm, 1)

        @block.vector
        def _(dve):
            order = Order(dve, dve_order)
            dve.memset(ones[:, :], 1.0).then_inc(ones_ready, 1)

            def tile_moments(kind, src, stats, b):
                tiles = list(range(STEPS))
                if kind == 1 and b == 0:
                    tiles = tiles[HALF:] + tiles[:HALF]
                for j in tiles:
                    if kind == 0 and b == 0 and j % HALF == 0:
                        dve.wait_ge(in_x[0] if j == 0 else in_x0_rest, 16)
                    if kind == 1 and j % HALF == 0:
                        if b == 0 and j == HALF:
                            dve.wait_ge(h0_ready, 1)
                        else:
                            dve.wait_ge(h_ready, H_READY[b][j // HALF])
                    ins = dve.bn_stats(stats[:, j, :], src(j))
                return ins

            def mean_variance(kind, stats, b):
                for j in range(STEPS):
                    ins = dve.bn_aggr(mean_var[:, j, :], stats[:, j, :])
                order.after(ins)
                dve.tensor_scalar(neg_mean[:, kind, b, :], mean_var[:, :, 0], -1.0, None, ALU.mult)
                dve.tensor_scalar(var[:, kind, b, :], mean_var[:, :, 1], LN_EPS, None, ALU.add
                                  ).then_inc(var_ready, 1)

            def second_norm(b):
                dve.wait_ge(rstd_ready, SECOND_RSTD[b])
                if b > 0:
                    dve.wait_ge(tr_done, 2 * b)
                for j in range(STEPS):
                    ins = dve.tensor_scalar(xn[:, j, :], hs[:, b, j, :], neg_mean[:, 1, b, j:j + 1],
                                            rstd[:, 1, b, j:j + 1], ALU.add, ALU.mult)
                    if j % HALF == HALF - 1:
                        ins.then_inc(xn_ready, 1)

            def first_moments(b):
                if b > 0:
                    dve.wait_ge(in_x[b], 16)
                order.after(tile_moments(0, lambda j: xs[:, b, j, :], st1, b))

            def conv_tap(b, m, s):
                if s == 1:
                    dve.wait_ge(xz_read, 8 * b + 2 * m + 2)
                else:
                    dve.wait_ge(tap_done, 2 * (2 * b + m) + s - 1)
                acc = conv[:, m, b].rearrange("p (j c) -> p j c", c=CH)
                dve.scalar_tensor_tensor(out=acc, in0=u[:, m, HALO - s:HALO - s + STEPS, :],
                                         scalar=conv_w[:, CONV_TAPS * (m + 1) - 1 - s:CONV_TAPS * (m + 1) - s],
                                         in1=acc, op0=ALU.mult, op1=ALU.add
                                         ).then_inc(tap_done if s < CONV_TAPS - 1 else conv_done, 1)

            def conv_taps(b, m):
                for s in range(1, CONV_TAPS):
                    conv_tap(b, m, s)

            dve.wait_ge(ones_ready, 1)
            dve.wait_ge(cond_ready, 1)
            for b in range(B):
                dve.tensor_scalar(cond_rows[:, b, :], ones[:, :], cond_s[:, b:b + 1], None, ALU.mult
                                  ).then_inc(cond_rows_ready, 1)
            for b in range(2):
                first_moments(b)
                mean_variance(0, st1, b)
            second = slice(HALF, STEPS)
            dve.wait_ge(rstd_ready, FIRST_RSTD[0])
            for j in range(HALF, STEPS):
                ins = dve.tensor_scalar(xhat[:, j, :], xs[:, 0, j, :], neg_mean[:, 0, 0, j:j + 1],
                                        rstd[:, 0, 0, j:j + 1], ALU.add, ALU.mult)
            order.after(ins)
            dve.wait_ge(mod_ready, 1)
            order.after(dve.tensor_tensor(hs[:, 0, second], xhat[:, second, :],
                                          scale_a[:, 0, :].unsqueeze(1).to_broadcast([P, HALF, D]), ALU.mult))
            dve.tensor_tensor(hs[:, 0, second], hs[:, 0, second],
                              shift_a[:, 0, :].unsqueeze(1).to_broadcast([P, HALF, D]), ALU.add
                              ).then_inc(h0_ready, 1)
            for b in range(B):
                if b == 1:
                    first_moments(3)
                    mean_variance(0, st1, 3)
                last = tile_moments(1, lambda j: hs[:, b, j, :], st2, b)
                if b > 0:
                    last.then_inc(moments_ready, 1)
                    conv_taps(b - 1, 0)
                else:
                    order.after(last)
                    mean_variance(1, st2, b)
                    first_moments(2)
                second_norm(b)
                if b == 0:
                    mean_variance(0, st1, 2)
                else:
                    conv_taps(b - 1, 1)

            def hold_gate(which, place):
                raw = gates[:, :, which * D:(which + 1) * D]
                sign, size = place[:, 0], place[:, 1]
                if which == 0:
                    dve.wait_ge(raw_ready, B)
                order.after(dve.tensor_scalar(sign, raw, 0.0, 2.0, ALU.is_ge, ALU.mult))
                order.after(dve.scalar_tensor_tensor(out=size, in0=sign, scalar=-1.0, in1=raw, op0=ALU.add,
                                                     op1=ALU.mult))
                order.after(dve.tensor_scalar(size, size, 0.25, None, ALU.max))
                dve.scalar_tensor_tensor(out=raw, in0=sign, scalar=-1.0, in1=size, op0=ALU.add,
                                         op1=ALU.mult).then_inc(gates_ready, 1)

            def gated_w_out(b):
                if b == 0:
                    dve.wait_ge(in_wout, 16)
                    dve.wait_ge(gates_ready, 1)
                for m in range(M):
                    ins = dve.scalar_tensor_tensor(out=wout_g[:, b, m, :], in0=wout_t[:, m, :], scalar=0.5,
                                                   in1=gates[:, b, 0:D], op0=ALU.mult, op1=ALU.mult)
                ins.then_inc(wout_ready, 1)

            def columns(t):
                return t[:, :, :].rearrange("p b C -> p (b C)")

            dve.wait_ge(scan_in, B)
            dve.tensor_copy(columns(y1), y_bank[:, :]).then_inc(scan_step, 1)
            hold_gate(0, gate_a_parts)
            dve.wait_ge(scan_mm, 1)
            dve.tensor_copy(columns(y2), small_bank[:, 0:16 * B]).then_inc(scan_step, 1)
            conv_tap(B - 1, 0, 1)
            conv_tap(B - 1, 0, 2)
            dve.wait_ge(scan_mm, 2)
            dve.tensor_copy(columns(y3), small_bank[:, 64:64 + 2 * B]).then_inc(scan_step, 1)
            gated_w_out(0)
            gated_w_out(1)
            gated_w_out(2)
            dve.wait_ge(scan_mm, 3)
            dve.tensor_tensor(y3[:, :, 1], y3[:, :, 1], small_bank[:, 76:76 + B], ALU.add).then_inc(scan_step, 1)
            gated_w_out(3)
            dve.wait_ge(scan_mm, 4)
            dve.wait_ge(const_ready, 10)
            dve.tensor_copy(carry2[:, :, 1:], small_bank[0:S, 128:128 + 16 * B].rearrange(
                "p (b C) -> p b C", b=B)[:, :, 1:]).then_inc(scan_step, 1)
            conv_tap(B - 1, 0, 3)
            dve.wait_ge(scan_mm, 5)
            dve.tensor_tensor(columns(y2), columns(y2), small_bank[:, 192:192 + 16 * B], ALU.add).then_inc(scan_step, 1)
            conv_tap(B - 1, 1, 1)
            dve.wait_ge(scan_mm, 6)
            dve.tensor_copy(carry1[:, :, 1:], tr_bank[0][0:S, :].rearrange("p (b C) -> p b C", b=B)[:, :, 1:]
                            ).then_inc(scan_step, 1)
            conv_tap(B - 1, 1, 2)
            dve.wait_ge(scan_mm, 7)
            dve.tensor_tensor(columns(y1), columns(y1), tr_bank[1][:, :], ALU.add).then_inc(state_ready, 1)
            conv_tap(B - 1, 1, 3)

            for n in range(UNITS + 1):
                if n < UNITS:
                    b, hf = n // 2, n % 2
                    cols = slice(hf * W, (hf + 1) * W)
                    dve.wait_ge(silu_done, 2 * (b + 1))
                    dve.wait_ge(xz_read, 8 * (b + 1))
                    for m in range(M):
                        dve.wait_ge(sc_mm, 2 * n + m + 1)
                        dve.tensor_tensor(conv[:, m, b, cols], conv[:, m, b, cols], sc_bank[m][:, :],
                                          ALU.add).then_inc(sc_read, 1)
                    if n >= 2:
                        dve.wait_ge(out_mm, n - 1)
                    for m in range(M):
                        dve.wait_ge(sc_read, 2 * n + m + 1)
                        dve.scalar_tensor_tensor(out=y[:, n % 2, m, :], in0=gate_z[:, m, b, cols], scalar=1.0,
                                                 in1=conv[:, m, b, cols], op0=ALU.add, op1=ALU.mult
                                                 ).then_inc(y_ready, 1)
                if 1 <= n <= UNITS:
                    k1 = n - 1
                    b, hf = k1 // 2, k1 % 2
                    dve.wait_ge(out_mm, k1 + 1)
                    dve.wait_ge(base_ready, b + 1)
                    rows = hs[:, b, hf * HALF:(hf + 1) * HALF, :].rearrange("p j d -> p (j d)")
                    dve.tensor_tensor(rows, rows, out_bank[:, :], ALU.add).then_inc(x1_ready, 1)
                    dve.wait_ge(x1_ready, k1 + 1)
                    if k1 >= 2:
                        dve.wait_ge(rstd_ready, 2 * B + k1 - 1)
                    for j in range(HALF):
                        ins = dve.bn_stats(st1[:, hf * HALF + j, :], hs[:, b, hf * HALF + j, :])
                    order.after(ins)
                    for j in range(HALF):
                        ins = dve.bn_aggr(mean_var[:, hf * HALF + j, :], st1[:, hf * HALF + j, :])
                    ins.then_inc(moments_ready, 1)

            dve.wait_ge(out_mm, UNITS)
            hold_gate(1, gate_b_parts)
            dve.wait_ge(const_ready, 13)
            order.after(dve.tensor_scalar(lane[:, :], lane[:, :], E, None, ALU.bitwise_and))
            order.after(dve.tensor_scalar(half_start[:, :], lane[:, :], float(L // 2 // E), None, ALU.mult))
            dve.wait_ge(logits_mm, 1)
            rounds = CAPACITY // 8
            for r in range(rounds):
                src = logit_bank[:, :] if r == 0 else left[(r - 1) % 2]
                eight = found[:, 8 * r:8 * r + 8]
                if r > 0:
                    dve.wait_ge(left_ready, r)
                order.after(dve.max(eight, src))
                if r == 0:
                    dve.tensor_scalar(neg_max[:, 0:1], found[:, 0:1], -1.0, None, ALU.mult).then_inc(max_ready, 1)
                if r + 1 < rounds:
                    dve.match_replace(left[r % 2], eight, src, LOWEST).then_inc(left_ready, 1)
                dve.max_index(found_at[:, 8 * r:8 * r + 8], eight, src).then_inc(index_ready, 1)
            dve.wait_ge(index_ready, rounds)
            dve.tensor_scalar(found[:, CAPACITY:], found_at[:, :], half_start[:, 0:1], None, ALU.add
                              ).then_inc(found_ready, 1)
            dve.wait_ge(other_mm, 1)
            other = other_bank[:, CAPACITY - 1::-1]
            other_token = other_bank[:, 2 * CAPACITY - 1:CAPACITY - 1:-1]
            dve.tensor_tensor(keep[:, :], found[:, 0:CAPACITY], other, ALU.is_ge)
            dve.tensor_tensor(best[:, :], found[:, 0:CAPACITY], other, ALU.max)
            order.after(dve.tensor_tensor(best_token[:, :], found[:, CAPACITY:], other_token, ALU.subtract))
            order.after(dve.tensor_tensor(best_token[:, :], best_token[:, :], keep[:, :], ALU.mult))
            dve.tensor_tensor(best_token[:, :], best_token[:, :], other_token, ALU.add).then_inc(weights_ready, 1)
            dve.tensor_copy(half_max[:, 0:1], found[:, 0:1])
            order.after(dve.tensor_copy(half_max[:, 1:2], other_bank[:, 0:1]))
            merged_at = dve.tensor_tensor(neg_max[:, 1:2], half_max[:, 0:1], half_max[:, 1:2], ALU.max)
            merged_at.then_inc(merged, 1)
            dve.wait_ge(slots_mm, 1)
            dve.wait_ge(const_ready, 12)
            dve.tensor_tensor(slot_row[:, :], slot_bank[0][:, 0:NG * B], batch_row[:, :, :].rearrange("p g b -> p (g b)"),
                              ALU.add).then_inc(slots_ready, 1)
            dve.tensor_copy(slot_at[:, 0, :], slot_bank[0][:, 0:NG * B])
            dve.wait_ge(merged, 1)
            dve.tensor_scalar(neg_max[:, 1:2], neg_max[:, 1:2], -1.0, None, ALU.mult).then_inc(max_ready, 1)
            dve.wait_ge(other_mm, 2)
            order.after(dve.tensor_copy(half_sum[:, 1:2], other_bank[:, 2 * CAPACITY:2 * CAPACITY + 1]))
            dve.wait_ge(exp_ready, 2)
            order.after(dve.tensor_tensor(exp_all[:, :], half_part[:, :], half_sum[:, :], ALU.mult))
            order.after(dve.tensor_tensor(exp_all[:, 0:1], exp_all[:, 0:1], exp_all[:, 1:2], ALU.add))
            order.after(dve.reciprocal(rz[:, :], exp_all[:, 0:1]))
            order.after(dve.tensor_scalar(den[:, :], exp_top[:, :], rz[:, 0:1], 1e-9, ALU.mult, ALU.add))
            order.after(dve.reciprocal(rden[:, :], den[:, :]))
            dve.tensor_scalar(w_top[:, :], e_top[:, :], rz[:, 0:1], rden[:, 0:1], ALU.mult, ALU.mult
                              ).then_inc(weights_ready, 1)
            dve.wait_ge(slots_mm, 2)
            dve.tensor_copy(slot_at[:, 1, :], slot_bank[1][:, 0:NG * B]).then_inc(slots_ready, 1)
            dve.wait_ge(slots_ready, 2)

            def one_hot(g, b):
                dve.tensor_scalar(onehot[:, g, b, :], token_of[:, :, :].rearrange("p j c -> p (j c)"),
                                  slot_at[:, 0, bass.ds(g * B + b, 1)], None, ALU.is_equal).then_inc(onehot_ready, 1)

            HOTS_FIRST = 2

            def expert_value(g):
                dve.wait_ge(eout_mm, g + 1)
                if g >= 1:
                    dve.wait_ge(lo_ready, g)
                else:
                    dve.wait_ge(gates_ready, 2)
                for b in range(B):
                    ins = dve.scalar_tensor_tensor(out=value[:, b, :], in0=eout_bank[:, b * D:(b + 1) * D],
                                                   scalar=slot_at[:, 1, g * B + b:g * B + b + 1],
                                                   in1=gates[:, b, D:2 * D], op0=ALU.mult, op1=ALU.mult)
                ins.then_inc(value_ready, 1)

            with dve.Fori(0, HOTS_FIRST) as g:
                for b in range(B):
                    one_hot(g, b)
            for e in range(E):
                g, q = e // G, e % G
                dve.wait_ge(silu_g_ready, e + 1)
                if g >= 2 and q == 0:
                    dve.wait_ge(eout_mm, g - 1)
                dve.tensor_tensor(hidden[g % 2][:, q].rearrange("p f t -> p (f t)"), silu_g[:, e % FFN_BUFS, :],
                                  ffn_bank[e % FFN_BUFS][:, FH * P:2 * FH * P], ALU.mult).then_inc(hidden_ready, 1)
                if e < B * (NG - HOTS_FIRST):
                    one_hot(HOTS_FIRST + e // B, e % B)
                if g >= 1 and q == 1:
                    expert_value(g - 1)
            expert_value(NG - 1)
            for n in range(UNITS - 1):
                b, hf = n // 2, n % 2
                dve.wait_ge(scatter_mm, n + 1)
                rows = hs[:, b, hf * HALF:(hf + 1) * HALF, :].rearrange("p j d -> p (j d)")
                dve.tensor_tensor(rows, rows, scatter_bank[n][:, :], ALU.add).then_inc(final_ready, 1)
            for part, src in enumerate(last_banks):
                dve.wait_ge(scatter_mm, UNITS + part)
                rows = hs[:, B - 1, HALF + part * PART:HALF + (part + 1) * PART, :].rearrange("p j d -> p (j d)")
                dve.tensor_tensor(rows, rows, src[:, part * PART * D:(part + 1) * PART * D], ALU.add
                                  ).then_inc(final_ready, 1)


def kernel(**inputs):
    import numpy as np
    import concourse.bacc as bacc
    from concourse.bass_utils import run_bass_kernel_spmd

    a = {n: np.ascontiguousarray(v) for n, v in inputs.items()}
    t = np.ascontiguousarray
    d = a["L0_attn_x"].shape[-1]
    inner = a["L0_attn_conv_w"].shape[0]
    m = inner // d
    vectors = np.concatenate([
        a["L0_c"].T, a["L0_attn_ln_gamma"][:, None], a["L0_attn_ln_beta"][:, None],
        a["L0_attn_conv_b"].reshape(m, d).T,
        a["L0_attn_conv_w"].reshape(m, d, -1).transpose(1, 0, 2).reshape(d, -1)], axis=1)
    arrays = dict(
        x=a["L0_attn_x"], vectors=t(vectors), w_mod=a["L0_wmod"],
        w_in_t=t(a["L0_attn_W_in"].T),
        w_in_x=t(a["L0_attn_W_in"][:inner].reshape(m, d, d).transpose(1, 0, 2)),
        w_out_t=t(a["L0_attn_W_out"].T.reshape(m, d, d).transpose(1, 0, 2)),
        a_pair=t(np.stack([a["L0_attn_A"], a["L0_attn_A"].T], axis=1)),
        c_m=a["L0_attn_Cm"],
        b_m_t=t(a["L0_attn_Bm"].T.reshape(m, d, -1).transpose(1, 0, 2)),
        router_w1=a["L0_ffn_router_w1"], router_w2=a["L0_ffn_router_w2"],
        w1=a["L0_ffn_w1"], w2=a["L0_ffn_w2"],
        w3=t(a["L0_ffn_w3"].reshape(a["L0_ffn_w3"].shape[0], -1, d, d).transpose(0, 2, 1, 3)),
    )
    nc = bacc.Bacc("TRN2", target_bir_lowering=False, num_devices=1)
    args = {n: nc.dram_tensor(f"in_{n}", v.shape, mybir.dt.from_np(v.dtype), kind="ExternalInput").ap()
            for n, v in arrays.items()}
    out = nc.dram_tensor("out_0", arrays["x"].shape, F32, kind="ExternalOutput").ap()
    adaln_block(nc, out=out, **args)
    r = run_bass_kernel_spmd(nc, [{f"in_{n}": v for n, v in arrays.items()}], core_ids=[0])
    return r.results[0]["out_0"]
```
